# Optimizing a Trainium2 kernel written in Bass

```python
import numpy as np
import jax
import jax.numpy as jnp

def _softmax(x, axis=-1):
    return jax.nn.softmax(x, axis=axis)

def _gelu(x):
    return jax.nn.gelu(x, approximate=True)

def _silu(x):
    return jax.nn.silu(x)

def _sigmoid(x):
    return jax.nn.sigmoid(x)

def _layernorm(x, axis=-1, eps=1e-05):
    m = jnp.mean(x, axis=axis, keepdims=True)
    v = jnp.var(x, axis=axis, keepdims=True)
    return (x - m) / jnp.sqrt(v + eps)

def _scatter_add(tgt, idx, src, axis=0):
    return tgt.at[idx].add(src)

def _segment_sum(src, seg, n):
    return jax.ops.segment_sum(src, seg, n)
kernel_name = 'mk_seq_postln_d1_jaxref_r4_38a46f'

def setup_inputs(seed: int=0):
    np.random.seed(seed)
    _w = jnp.asarray

    def _L0_attn_setup():
        import jax, jax.numpy as jnp
        import numpy as np
        H, KV, D = (8, 2, 64)
        RD = D // 4
        ROPE_THETA = 10000.0

        def _rope_cos_sin(seq_len, dtype):
            inv_freq = 1.0 / ROPE_THETA ** (jnp.arange(0, RD, 2, dtype=jnp.float32) / RD)
            pos = jnp.arange(seq_len, dtype=jnp.float32)
            freqs = pos[:, None] * inv_freq[None, :]
            emb = jnp.concatenate([freqs, freqs], axis=-1)
            return (jnp.cos(emb).astype(dtype), jnp.sin(emb).astype(dtype))

        def _apply_partial_rope(x, cos, sin):
            x_rot, x_pass = (x[..., :RD], x[..., RD:])
            half = RD // 2
            rot = jnp.concatenate([-x_rot[..., half:], x_rot[..., :half]], axis=-1)
            x_rot = x_rot * cos[None, None] + rot * sin[None, None]
            return jnp.concatenate([x_rot, x_pass], axis=-1)
        key = jax.random.key(seed)
        ks = jax.random.split(key, 5)
        B, S, hid = (4, 512, 256)
        s = 0.02
        return {'hidden_states': jax.random.normal(ks[0], (B, S, hid), jnp.float32), 'Wq': jax.random.normal(ks[1], (hid, H * D * 2), jnp.float32) * s, 'Wk': jax.random.normal(ks[2], (hid, KV * D), jnp.float32) * s, 'Wv': jax.random.normal(ks[3], (hid, KV * D), jnp.float32) * s, 'Wo': jax.random.normal(ks[4], (H * D, hid), jnp.float32) * s}
    _L0_attn_in = _L0_attn_setup()

    def _L0_ffn_setup():
        import jax, jax.numpy as jnp
        import numpy as np

        def _bitlinear(x, w_latent):
            scale = jax.lax.stop_gradient(jnp.clip(jnp.mean(jnp.abs(w_latent), axis=1, keepdims=True), 1e-05, None))
            tern = jnp.clip(jnp.round(w_latent / scale), -1.0, 1.0)
            w = w_latent + jax.lax.stop_gradient(tern - w_latent)
            return x @ (w * scale).T
        key = jax.random.key(seed)
        ks = jax.random.split(key, 6)
        dim, hidden, rank = (256, 1024, 16)
        B, S = (4, 1024)
        x = jax.random.normal(ks[0], (B, S, dim), dtype=jnp.float32)
        w_fc = 0.02 * jax.random.normal(ks[1], (hidden, dim), dtype=jnp.float32)
        w_proj = 0.02 * jax.random.normal(ks[2], (dim, hidden), dtype=jnp.float32)
        u = 0.02 * jax.random.normal(ks[3], (hidden, rank), dtype=jnp.float32)
        v = 0.02 * jax.random.normal(ks[4], (rank, dim), dtype=jnp.float32)
        fast_b = jax.random.normal(ks[5], (rank, rank), dtype=jnp.float32)
        gate = jnp.float32(0.05)
        return {'x': x, 'fast_b': fast_b, 'w_fc': w_fc, 'w_proj': w_proj, 'u': u, 'v': v, 'gate': gate}
    _L0_ffn_in = _L0_ffn_setup()
    _d = {'L0_attn_hidden_states': _L0_attn_in['hidden_states'], 'L0_attn_Wq': _L0_attn_in['Wq'], 'L0_attn_Wk': _L0_attn_in['Wk'], 'L0_attn_Wv': _L0_attn_in['Wv'], 'L0_attn_Wo': _L0_attn_in['Wo'], 'L0_ffn_fast_b': _L0_ffn_in['fast_b'], 'L0_ffn_w_fc': _L0_ffn_in['w_fc'], 'L0_ffn_w_proj': _L0_ffn_in['w_proj'], 'L0_ffn_u': _L0_ffn_in['u'], 'L0_ffn_v': _L0_ffn_in['v'], 'L0_ffn_gate': _L0_ffn_in['gate']}
    _x0 = _d['L0_attn_hidden_states']
    _d['L0_attn_hidden_states'] = jax.random.normal(jax.random.fold_in(jax.random.key(seed), 1), (2, 2048, 256), dtype=_x0.dtype)
    del _x0
    return _d

def reference(L0_attn_hidden_states, L0_attn_Wq, L0_attn_Wk, L0_attn_Wv, L0_attn_Wo, L0_ffn_fast_b, L0_ffn_w_fc, L0_ffn_w_proj, L0_ffn_u, L0_ffn_v, L0_ffn_gate):

    def _L0_attn_ref(hidden_states, Wq, Wk, Wv, Wo):
        import jax, jax.numpy as jnp
        import numpy as np
        H, KV, D = (8, 2, 64)
        RD = D // 4
        ROPE_THETA = 10000.0

        def _rope_cos_sin(seq_len, dtype):
            inv_freq = 1.0 / ROPE_THETA ** (jnp.arange(0, RD, 2, dtype=jnp.float32) / RD)
            pos = jnp.arange(seq_len, dtype=jnp.float32)
            freqs = pos[:, None] * inv_freq[None, :]
            emb = jnp.concatenate([freqs, freqs], axis=-1)
            return (jnp.cos(emb).astype(dtype), jnp.sin(emb).astype(dtype))

        def _apply_partial_rope(x, cos, sin):
            x_rot, x_pass = (x[..., :RD], x[..., RD:])
            half = RD // 2
            rot = jnp.concatenate([-x_rot[..., half:], x_rot[..., :half]], axis=-1)
            x_rot = x_rot * cos[None, None] + rot * sin[None, None]
            return jnp.concatenate([x_rot, x_pass], axis=-1)
        B, S, _ = hidden_states.shape
        G = H // KV
        qg = hidden_states @ Wq
        q, gate = (qg[..., :H * D], qg[..., H * D:])
        k = hidden_states @ Wk
        v = hidden_states @ Wv
        q = q.reshape(B, S, H, D).transpose(0, 2, 1, 3)
        k = k.reshape(B, S, KV, D).transpose(0, 2, 1, 3)
        v = v.reshape(B, S, KV, D).transpose(0, 2, 1, 3)
        cos, sin = _rope_cos_sin(S, q.dtype)
        q = _apply_partial_rope(q, cos, sin)
        k = _apply_partial_rope(k, cos, sin)
        qg4 = q.reshape(B, KV, G, S, D)
        scores = jnp.einsum('bkgsd,bktd->bkgst', qg4, k) / jnp.sqrt(jnp.asarray(D, q.dtype))
        attn = jax.nn.softmax(scores, axis=-1)
        out = jnp.einsum('bkgst,bktd->bkgsd', attn, v)
        out = out.reshape(B, H, S, D).transpose(0, 2, 1, 3).reshape(B, S, H * D)
        out = out * jax.nn.silu(gate)
        return out @ Wo

    def _L0_ffn_ref(x, fast_b, w_fc, w_proj, u, v, gate):
        import jax, jax.numpy as jnp
        import numpy as np

        def _bitlinear(x, w_latent):
            scale = jax.lax.stop_gradient(jnp.clip(jnp.mean(jnp.abs(w_latent), axis=1, keepdims=True), 1e-05, None))
            tern = jnp.clip(jnp.round(w_latent / scale), -1.0, 1.0)
            w = w_latent + jax.lax.stop_gradient(tern - w_latent)
            return x @ (w * scale).T
        h = _bitlinear(x, w_fc) + gate * (x @ v.T @ fast_b.T @ u.T)
        r = jnp.maximum(h, 0.0)
        return _bitlinear(r * r, w_proj)
    x = L0_attn_hidden_states
    x = _layernorm(x + _L0_attn_ref(x, L0_attn_Wq, L0_attn_Wk, L0_attn_Wv, L0_attn_Wo), axis=-1)
    x = _layernorm(x + _L0_ffn_ref(x, L0_ffn_fast_b, L0_ffn_w_fc, L0_ffn_w_proj, L0_ffn_u, L0_ffn_v, L0_ffn_gate), axis=-1)
    return x

_drawn_inputs = setup_inputs


def setup_inputs(seed=0):
    import zlib

    import numpy as np

    out = dict(_drawn_inputs(seed))
    spreads = {}
    factors = {'L0_attn_Wq': 8.0,
     'L0_attn_Wk': 8.0,
     'L0_attn_Wv': 8.0,
     'L0_attn_Wo': 8.0,
     'L0_ffn_fast_b': 8.0,
     'L0_ffn_u': 8.0,
     'L0_ffn_v': 8.0}
    for name, (base, spread) in spreads.items():
        noise = np.random.default_rng([zlib.crc32(name.encode()), seed]).standard_normal(out[name].shape)
        drawn = base * np.exp(spread * noise) if base else spread * noise
        out[name] = jnp.asarray(drawn.astype(out[name].dtype))
    for name, factor in factors.items():
        out[name] = (out[name] * factor).astype(out[name].dtype)
    return out
```

```python
from contextlib import ExitStack

import numpy as np

import concourse.bass as bass
from concourse import mybir

F32 = mybir.dt.float32
F32R = mybir.dt.float32r
ALU = mybir.AluOpType
ACT = mybir.ActivationFunctionType
AX_X = mybir.AxisListType.X

P = 128
BATCH, SEQ, HID = 2, 2048, 256
HEADS, KVH, D = 8, 2, 64
ROT = D // 4
FFN, RANK = 1024, 16
EPS = 1e-5
CHUNK = 512
NCH = SEQ // CHUNK
PAIRS = HEADS // 2
UNITS = NCH * PAIRS
STEPS = SEQ // P
HC = HID // P
KEYCH = SEQ // CHUNK
TILES = CHUNK // P
MAXES = 2 * TILES * KEYCH
JT = FFN // P
STAGES = NCH + UNITS
RING = 4
LEAD = 12
HEAD = 6
AHEAD = 3
PRIME = 4


def done(n):
    return n + PRIME


def attention_steps(eng, emit):
    for k in range(HEAD):
        emit(0, k)
    with eng.Fori(0, NCH - 1) as c:
        for k in range(HEAD, HEAD + PAIRS * STEPS):
            emit(c, k)
    for k in range(HEAD, PAIRS * STEPS):
        emit(NCH - 1, k)


def first(c, p):
    return isinstance(c, int) and c == 0 and p == 0


def exists(c, p, ahead):
    return not (isinstance(c, int) and c == NCH - 1 and p + ahead >= PAIRS)


def layer_kernel(nc, x, xT, wq, wk, wv, wo, fast_bT, w_fc, w_proj, uT, v_lr, gate, cos_t, sin_t, ident_in, out):
    ctx = ExitStack()
    with ctx:
        def sb(name, shape, dt=F32):
            return ctx.enter_context(nc.sbuf_tensor(name, shape, dt))

        def ps(name, shape):
            return ctx.enter_context(nc.psum_tensor(name, shape, F32))

        def sem(name):
            return ctx.enter_context(nc.semaphore(name))

        wqg_sb = sb("wqg_sb", [P, HC, 2 * HEADS * D])
        wk_sb = sb("wk_sb", [P, HC, P])
        wv_sb = sb("wv_sb", [P, HC, P])
        wo_sb = sb("wo_sb", [P, PAIRS, HID])
        wfcT = sb("wfcT", [P, HC, FFN])
        wpT = sb("wpT", [P, JT, HID])
        ident = sb("ident", [P, P])
        ones = sb("ones", [P, D])
        gate_sb = sb("gate_sb", [P, 1])
        xT_sb = sb("xT_sb", [P, HC, SEQ])
        ka = sb("ka", [P, KVH, SEQ], F32R)
        kb = sb("kb", [P, KVH, SEQ], F32R)
        v_sb = sb("v_sb", [P, STEPS, P])
        qa = sb("qa", [P, PAIRS, 2, CHUNK], F32R)
        qb = sb("qb", [P, PAIRS, 2, CHUNK], F32R)
        og = sb("og", [P, UNITS, CHUNK])
        cos_sb = sb("cos_sb", [P, 2, CHUNK])
        sin_sb = sb("sin_sb", [P, 2, CHUNK])
        raw = sb("raw", [P, 2, CHUNK])
        rot = sb("rot", [P, 2, CHUNK])
        high = sb("high", [P, 2, CHUNK], F32R)
        low = sb("low", [P, 2, CHUNK], F32R)
        probs = sb("probs", [P, RING, 2 * CHUNK])
        acc = sb("acc", [P, 2, 2 * CHUNK])
        maxp = sb("maxp", [P, 2, MAXES])
        max8 = sb("max8", [P, 2 * TILES])
        mrow = sb("mrow", [2 * TILES, P], F32R)
        o_sb = sb("o_sb", [P, CHUNK])
        g_sb = sb("g_sb", [P, CHUNK])
        e_sb = sb("e_sb", [P, CHUNK])
        stats = sb("stats", [P, TILES, 6])
        mv = sb("mv", [P, TILES, 2])
        var_eps = sb("var_eps", [P, TILES])
        std = sb("std", [P, TILES])
        rstd = sb("rstd", [P, TILES])
        scales = sb("scales", [P, 3, JT + HC])

        attnT = raw[:, :, :]
        x1T = rot[:, :, :]
        y1 = high[:, :, :].bitcast(F32).rearrange("p a (b c) -> p (a b) c", c=HID)
        x1 = low[:, :, :].bitcast(F32).rearrange("p a (b c) -> p (a b) c", c=HID)
        xres = acc[:, 0, :].rearrange("p (i c) -> p i c", c=HID)
        yout = acc[:, 1, :].rearrange("p (i c) -> p i c", c=HID)
        rr = probs[:, :, :].rearrange("p r (a n) -> p (r a) n", n=CHUNK)
        wfc_nat = og[:, 0:4, :].rearrange("p a (b c) -> p (a b) c", c=HID)
        wfc_w = og[:, 4:8, :].rearrange("p a (b c) -> p (a b) c", c=HID)
        wp_nat = og[:, 8:12, :].rearrange("p (a b) c -> p a (b c)", a=HC)
        wp_w = og[:, 12:16, :].rearrange("p (a b) c -> p a (b c)", a=HC)
        uT_sb = probs[0:RANK, 0, :]
        v_lr_sb = probs[0:RANK, 1, 0:HID]
        fbT_sb = probs[0:RANK, 2, 0:RANK]
        bv_sb = probs[0:RANK, 3, 0:HID]

        sc = ps("sc", [P, 4, CHUNK])
        mx = ps("mx", [P, 2, CHUNK])
        ob = ps("ob", [P, CHUNK])
        misc = ps("misc", [P, CHUNK])

        weights_loaded = sem("weights_loaded")
        setup_pe = sem("setup_pe")
        setup_act = sem("setup_act")
        setup_dve = sem("setup_dve")
        ones_set = sem("ones_set")
        xT_loaded = sem("xT_loaded")
        tables_loaded = [sem(f"tables_loaded{i}") for i in range(2)]
        rot_placed = [sem(f"rot_placed{i}") for i in range(2)]
        placed = [sem(f"placed{i}") for i in range(2)]
        m_placed = sem("m_placed")
        xres_loaded = sem("xres_loaded")
        y_stored = sem("y_stored")

        q_ready = sem("q_ready")
        v_ready = sem("v_ready")
        max_ready = sem("max_ready")
        mt_ready = sem("mt_ready")
        scores_ready = sem("scores_ready")
        pv_done = sem("pv_done")
        den_ready = sem("den_ready")
        gate_ready = sem("gate_ready")
        attn_ready = sem("attn_ready")
        tr_ready = sem("tr_ready")
        x1t_ready = sem("x1t_ready")
        ffn1_ready = sem("ffn1_ready")
        ffn2_ready = sem("ffn2_ready")
        PE_SEMS = [q_ready, v_ready, max_ready, mt_ready, scores_ready, pv_done, den_ready, gate_ready,
                   attn_ready, tr_ready, x1t_ready, ffn1_ready, ffn2_ready]

        q_copied = sem("q_copied")
        v_copied = sem("v_copied")
        rounded = [sem(f"rounded{i}") for i in range(2)]
        probs_ready = sem("probs_ready")
        gate_copied = sem("gate_copied")
        o_copied = sem("o_copied")
        attn_copied = sem("attn_copied")
        x1t_copied = sem("x1t_copied")
        relu_done = sem("relu_done")
        std_done = sem("std_done")
        ACT_SEMS = [q_copied, v_copied, *rounded, probs_ready, gate_copied, o_copied, attn_copied,
                    x1t_copied, relu_done, std_done]

        maxed = sem("maxed")
        max8_done = sem("max8_done")
        m_copied = sem("m_copied")
        sum_b = sem("sum_b")
        den_used = sem("den_used")
        recip_done = sem("recip_done")
        ln_chain = sem("ln_chain")
        res_done = sem("res_done")
        y2_done = sem("y2_done")
        var_ready = sem("var_ready")
        x1_done = sem("x1_done")
        post_done = sem("post_done")
        DVE_SEMS = [maxed, max8_done, m_copied, sum_b, den_used, recip_done, ln_chain, res_done,
                    y2_done, var_ready, x1_done, post_done]

        sum_a = sem("sum_a")
        og_step = sem("og_step")
        squared = sem("squared")
        rope_step = [sem(f"rope_step{i}") for i in range(2)]
        low_done = [sem(f"low_done{i}") for i in range(2)]
        POOL_SEMS = [sum_a, og_step, squared, *rope_step, *low_done]

        x_tiles = x.rearrange("(n i p) c -> p n i c", p=P, i=TILES)
        out_tiles = out.rearrange("(n i p) c -> p n i c", p=P, i=TILES)
        xT_v = xT.rearrange("(h p) t -> p h t", p=P)

        def occurrence(b, s_const, c=0):
            return b * (STAGES // 2) + c * (PAIRS // 2) + s_const // 2

        PRO = NCH + AHEAD

        def rope(eng, s_const, b, c=0):
            par, i = s_const % 2, occurrence(b, s_const, c)
            eng.wait_ge(rot_placed[par], 64 * (i + 1))
            eng.wait_ge(tables_loaded[par], 32 * (i + 1))
            eng.tensor_tensor(raw[:, par, :], raw[:, par, :], cos_sb[:, par, :], ALU.mult)\
               .then_inc(rope_step[par], 1)
            eng.tensor_tensor(rot[:, par, :], rot[:, par, :], sin_sb[:, par, :], ALU.mult)\
               .then_inc(rope_step[par], 1)

        def rope_add(eng, s_const, b, c=0):
            par, i = s_const % 2, occurrence(b, s_const, c)
            eng.wait_ge(rope_step[par], done(3 * i + 2))
            eng.tensor_tensor(raw[:, par, :], raw[:, par, :], rot[:, par, :], ALU.add)\
               .then_inc(rope_step[par], 1)

        def rope_low(eng, s_const, b, c=0):
            par, i = s_const % 2, occurrence(b, s_const, c)
            eng.wait_ge(rounded[par], done(i + 1))
            eng.wait_ge(placed[par], 96 * (i + 1))
            eng.tensor_tensor(low[:, par, :], raw[:, par, :], high[:, par, :].bitcast(F32), ALU.subtract)\
               .then_inc(low_done[par], 1)

        def add_exponentials(eng, ops, b, c, k, hd, summed):
            p, t = k // STEPS, k % STEPS
            n = (b * UNITS + c * PAIRS) * STEPS + k
            cols = slice(hd * CHUNK, (hd + 1) * CHUNK)
            total, part = acc[:, p % 2, cols], probs[:, k % RING, cols]
            if t == 1:
                eng.wait_ge(probs_ready, done(n + 1))
                eng.wait_ge(den_ready, done(b * UNITS + c * PAIRS + p - 1))
                ops.tensor_tensor(total, probs[:, (k - 1) % RING, cols], part, ALU.add).then_inc(summed, 2)
            elif t > 1:
                eng.wait_ge(probs_ready, done(n + 1))
                eng.wait_ge(summed, done(n))
                ops.tensor_tensor(total, total, part, ALU.add).then_inc(summed, 1)

        block = ctx.enter_context(nc.Block())

        @block.sync
        def _(sp):
            sp.sem_inc(m_placed, 16)
            for par in range(2):
                sp.sem_inc(placed[par], 96)
            sp.dma_start(wfc_nat, w_fc.rearrange("(j p) c -> p j c", p=P)).then_inc(weights_loaded, 16)
            sp.dma_start(wp_nat, w_proj.rearrange("(h p) j -> p h j", p=P)).then_inc(weights_loaded, 16)
            sp.dma_start(uT_sb, uT).then_inc(weights_loaded, 16)
            sp.dma_start(v_lr_sb, v_lr).then_inc(weights_loaded, 16)
            sp.dma_start(fbT_sb, fast_bT).then_inc(weights_loaded, 16)
            sp.dma_start(gate_sb[:, :], gate).then_inc(weights_loaded, 16)
            sp.dma_start(ident[:, :], ident_in).then_inc(weights_loaded, 16)
            sp.dma_start(wqg_sb[:, :, :], wq.rearrange("(h p) n -> p h n", p=P)).then_inc(weights_loaded, 16)
            sp.dma_start(wk_sb[:, :, :], wk.rearrange("(h p) n -> p h n", p=P)).then_inc(weights_loaded, 16)
            sp.dma_start(wv_sb[:, :, :], wv.rearrange("(h p) n -> p h n", p=P)).then_inc(weights_loaded, 16)
            sp.dma_start(wo_sb[:, :, :], wo.rearrange("(h p) n -> p h n", p=P)).then_inc(weights_loaded, 16)

            def tables(s_const, b, chunk, c=0):
                par, i = s_const % 2, occurrence(b, s_const, c)
                sp.wait_ge(low_done[par], done(i))
                for dst, src in ((cos_sb, cos_t), (sin_sb, sin_t)):
                    sp.dma_start(dst[:, par, :], src[:, bass.ds(chunk * CHUNK, CHUNK)])\
                      .then_inc(tables_loaded[par], 16)

            def swap_rows(s_const, b, c=0):
                par, h = s_const % 2, ROT // 2
                sp.wait_ge(q_copied, done(b * STAGES + c * PAIRS + s_const + 1))
                for base in (0, D):
                    for to, frm in ((base, base + h), (base + h, base)):
                        sp.dma_start(rot[to:to + h, par, :], raw[frm:frm + h, par, :])\
                          .then_inc(rot_placed[par], 16)

            def place(s_const, b, targets, c=0):
                par, i = s_const % 2, occurrence(b, s_const, c)
                sp.wait_ge(low_done[par], done(i + 1))
                for part, hd, dst in targets:
                    sp.dma_start(raw_words(dst), raw_words(part[hd * D:(hd + 1) * D, par, :]))\
                      .then_inc(placed[par], 16)

            def k_targets(n):
                keys = slice(n * CHUNK, (n + 1) * CHUNK)
                return [t for g in range(KVH) for t in (
                    (high, g, ka[0:D, g, keys]), (low, g, ka[D:P, g, keys]), (high, g, kb[0:D, g, keys]))]

            def q_targets(slot):
                return [t for hd in range(2) for t in (
                    (high, hd, qa[0:D, slot, hd, :]), (high, hd, qa[D:P, slot, hd, :]), (low, hd, qb[0:D, slot, hd, :]))]

            def place_max(b, c, p):
                sp.wait_ge(m_copied, done(b * UNITS + c * PAIRS + p + 1))
                sp.dma_start(raw_words(qb[D:D + 1, p % PAIRS, :, :]), raw_words(mrow[:, :])).then_inc(m_placed, 16)

            def step(b):
                def emit(c, k):
                    p, t = k // STEPS, k % STEPS
                    unit = b * UNITS + c * PAIRS + p
                    s_const = NCH + AHEAD + p
                    if t == 3 and has_q(c, p):
                        tables(s_const, b, c + (p + AHEAD) // PAIRS, c)
                    if t == 5 and has_q(c, p):
                        swap_rows(s_const, b, c)
                    if t == 11 and has_q(c, p):
                        place(s_const, b, q_targets((p + AHEAD) % PAIRS), c)
                    if t == 13 and exists(c, p, 1):
                        place_max(b, c, p + 1)
                return emit

            with sp.Fori(0, BATCH) as b:
                sp.wait_ge(gate_ready, done(b * UNITS))
                sp.dma_start(xT_sb[:, :, :], xT_v[:, :, bass.ds(b * SEQ, SEQ)]).then_inc(xT_loaded, 16)
                sp.wait_ge(ones_set, 3)
                sp.wait_ge(post_done, done(b * NCH))
                chunk_of = [*range(NCH)] + [0] * AHEAD
                tables(0, b, 0)
                tables(1, b, 1)
                swap_rows(0, b)
                for s in range(PRO):
                    if s + 1 < PRO:
                        swap_rows(s + 1, b)
                    place(s, b, k_targets(s) if s < NCH else q_targets(s - NCH))
                    if s + 2 < PRO:
                        tables(s + 2, b, chunk_of[s + 2])
                place_max(b, 0, 0)
                attention_steps(sp, step(b))
                with sp.Fori(0, NCH) as c:
                    sp.wait_ge(og_step, done(2 * UNITS * (b + 1)))
                    sp.wait_ge(res_done, done((b * NCH + c) * TILES))
                    sp.dma_start(xres, x_tiles[:, b * NCH + c, :, :]).then_inc(xres_loaded, 16)
                    sp.wait_ge(post_done, done(b * NCH + c + 1))
                    sp.dma_start(out_tiles[:, b * NCH + c, :, :], yout).then_inc(y_stored, 16)
            sp.wait_ge(y_stored, 16 * BATCH * NCH)

        @block.tensor
        def _(pe):
            for s in PE_SEMS:
                pe.sem_inc(s, PRIME)

            pe.wait_ge(weights_loaded, 16 * 11)
            nc.tensor.matmul(misc[0:RANK, 0:HID], fbT_sb, v_lr_sb, start=True, stop=True).then_inc(setup_pe, 1)
            pe.wait_ge(setup_act, 1)
            for j in range(JT):
                mm = nc.tensor.matmul(sc[:, j // 2, (j % 2) * HID:(j % 2 + 1) * HID],
                                      uT_sb[:, j * P:(j + 1) * P], bv_sb, start=True, stop=True)
            mm.then_inc(setup_pe, 1)
            pe.wait_ge(setup_dve, 1)
            banks = [mx[:, 0, :], mx[:, 1, :], ob[:, :], misc[:, :]]
            for h in range(HC):
                for j in range(JT):
                    tr = nc.tensor.transpose(banks[2 * h + j // 4][:, (j % 4) * P:(j % 4 + 1) * P],
                                             wfc_w[:, j, h * P:(h + 1) * P], ident[:, :])
            tr.then_inc(setup_pe, 1)
            pe.wait_ge(setup_dve, 2)
            for j in range(JT):
                for h in range(HC):
                    tr = nc.tensor.transpose(sc[:, j // 2, (j % 2) * HID + h * P:(j % 2) * HID + (h + 1) * P],
                                             wp_w[:, h, j * P:(j + 1) * P], ident[:, :])
            tr.then_inc(setup_pe, 1)
            pe.wait_ge(setup_act, 3)

            def project(w, col, chunk, semaphore):
                for h in range(HC):
                    mm = nc.tensor.matmul(misc[:, :], w[:, h, col:col + P],
                                          xT_sb[:, h, bass.ds(chunk * CHUNK, CHUNK)],
                                          start=(h == 0), stop=(h == HC - 1))
                mm.then_inc(semaphore, 1)

            def v_group(g, b):
                for i in range(TILES):
                    tile = g * TILES + i
                    for h in range(HC):
                        mm = nc.tensor.matmul(sc[:, g, i * P:(i + 1) * P], xT_sb[:, h, tile * P:(tile + 1) * P],
                                              wv_sb[:, h, :], start=(h == 0), stop=(h == HC - 1))
                mm.then_inc(v_ready, 1)

            def row_max(b, c, p, j):
                hd, st, kc = j // (TILES * KEYCH), j // KEYCH % TILES, j % KEYCH
                unit = b * UNITS + c * PAIRS + p
                if j == 0:
                    s = NCH + p
                    pe.wait_ge(placed[s % 2], 96 * (occurrence(b, s, c) + 2))
                pe.wait_ge(maxed, done(unit * MAXES + j - 1))
                nc.tensor.matmul(mx[:, j % 2, :], qa[:, p % PAIRS, hd, st * P:(st + 1) * P],
                                 ka[:, p % PAIRS // 2, kc * CHUNK:(kc + 1) * CHUNK],
                                 start=True, stop=True).then_inc(max_ready, 1)

            def max_transpose(b, c, p):
                pe.wait_ge(max8_done, done(b * UNITS + c * PAIRS + p + 1))
                nc.tensor.transpose(misc[0:2 * TILES, 0:P], max8[:, :], ident[:, :]).then_inc(mt_ready, 1)

            def scores(b, c, k):
                p, t = k // STEPS, k % STEPS
                n = (b * UNITS + c * PAIRS) * STEPS + k
                keys, kv = slice(t * P, (t + 1) * P), p % PAIRS // 2
                if t == 0:
                    pe.wait_ge(m_placed, 16 * (b * UNITS + c * PAIRS + p + 2))
                pe.wait_ge(probs_ready, done(n - 1))
                for hd in range(2):
                    nc.tensor.matmul(sc[:, 2 * (k % 2) + hd, :], ka[:, kv, keys], qa[:, p % PAIRS, hd, :],
                                     start=True, stop=False)
                for hd in range(2):
                    mm = nc.tensor.matmul(sc[:, 2 * (k % 2) + hd, :], kb[0:D + 1, kv, keys],
                                          qb[0:D + 1, p % PAIRS, hd, :], start=False, stop=True)
                mm.then_inc(scores_ready, 1)

            def weighted_v(b, c, k):
                p, t = k // STEPS, k % STEPS
                n = (b * UNITS + c * PAIRS) * STEPS + k
                kv = p % PAIRS // 2
                pe.wait_ge(probs_ready, done(n + 1))
                if t == 0:
                    pe.wait_ge(o_copied, done(b * UNITS + c * PAIRS + p))
                for hd in range(2):
                    mm = nc.tensor.matmul(ob[hd * D:(hd + 1) * D, :], v_sb[:, t, kv * D:(kv + 1) * D],
                                          probs[:, k % RING, hd * CHUNK:(hd + 1) * CHUNK],
                                          start=(t == 0), stop=(t == STEPS - 1))
                mm.then_inc(pv_done, 1)

            def denominators(b, c, p):
                unit = b * UNITS + c * PAIRS + p
                pe.wait_ge(sum_a, done((unit + 1) * STEPS))
                pe.wait_ge(sum_b, done((unit + 1) * STEPS))
                for hd in range(2):
                    mm = nc.tensor.matmul(misc[hd * D:(hd + 1) * D, :], ones[:, :],
                                          acc[:, p % 2, hd * CHUNK:(hd + 1) * CHUNK], start=True, stop=True)
                mm.then_inc(den_ready, 1)

            def step(b):
                def emit(c, k):
                    p, t = k // STEPS, k % STEPS
                    unit = b * UNITS + c * PAIRS + p
                    if not (isinstance(c, int) and c == NCH - 1 and k == PAIRS * STEPS - 1):
                        scores(b, c, k + 1)
                    for j in (LEAD + 2 * t, LEAD + 2 * t + 1):
                        ahead = 1 + j // MAXES
                        if exists(c, p, ahead):
                            row_max(b, c, p + ahead, j % MAXES)
                    weighted_v(b, c, k)
                    if t == 2 and not first(c, p):
                        pe.wait_ge(m_copied, done(unit + 1))
                        denominators(b, c, p - 1)
                    if t == 4 and has_q(c, p):
                        if first(c, p):
                            pe.wait_ge(m_copied, done(unit + 1))
                        else:
                            pe.wait_ge(den_used, done(unit))
                        project(wqg_sb, (p + AHEAD) % PAIRS * P, c + (p + AHEAD) // PAIRS, q_ready)
                    if t == 7:
                        if has_q(c, p):
                            pe.wait_ge(q_copied, done(b * STAGES + c * PAIRS + PRO + p + 1))
                        else:
                            pe.wait_ge(den_used, done(unit))
                        project(wqg_sb, HEADS * D + p % PAIRS * P, c, gate_ready)
                    if t == 11 and exists(c, p, 1):
                        pe.wait_ge(gate_copied, done(unit + 1))
                        max_transpose(b, c, p + 1)
                return emit

            def rest(b, c):
                n = b * NCH + c
                pe.wait_ge(og_step, done(2 * UNITS * (b + 1)))
                pe.wait_ge(relu_done, done(n * JT))
                for h in range(HC):
                    for p in range(PAIRS):
                        mm = nc.tensor.matmul(sc[:, h, :], wo_sb[:, p, h * P:(h + 1) * P],
                                              og[:, c * PAIRS + p, :], start=(p == 0), stop=(p == PAIRS - 1))
                    mm.then_inc(attn_ready, 1)
                pe.wait_ge(attn_copied, done((n + 1) * HC))
                pe.wait_ge(res_done, done(n * TILES))
                for i in range(TILES):
                    for h in range(HC):
                        tr = nc.tensor.transpose(sc[:, 2 + i // 2, (i % 2) * HID + h * P:(i % 2) * HID + (h + 1) * P],
                                                 attnT[:, h, i * P:(i + 1) * P], ident[:, :])
                    if i % 2:
                        tr.then_inc(tr_ready, 1)
                pe.wait_ge(x1_done, done((n + 1) * TILES))
                pe.wait_ge(x1t_copied, done(n * HC))
                for h in range(HC):
                    for i in range(TILES):
                        tr = nc.tensor.transpose(mx[:, h, i * P:(i + 1) * P], x1[:, i, h * P:(h + 1) * P], ident[:, :])
                    tr.then_inc(x1t_ready, 1)
                pe.wait_ge(x1t_copied, done((n + 1) * HC))
                for j in range(JT):
                    if j >= 2:
                        pe.wait_ge(relu_done, done(n * JT + j - 1))
                    for h in range(HC):
                        mm = nc.tensor.matmul(sc[:, j % 2, :], wfcT[:, h, j * P:(j + 1) * P], x1T[:, h, :],
                                              start=(h == 0), stop=(h == HC - 1))
                    mm.then_inc(ffn1_ready, 1)
                pe.wait_ge(squared, done((n + 1) * JT))
                pe.wait_ge(y2_done, done(n * TILES))
                for i in range(TILES):
                    bank = (ob if i < 2 else misc)[:, (i % 2) * HID:(i % 2 + 1) * HID]
                    for j in range(JT):
                        mm = nc.tensor.matmul(bank, rr[:, j, i * P:(i + 1) * P], wpT[:, j, :],
                                              start=(j == 0), stop=(j == JT - 1))
                    if i % 2:
                        mm.then_inc(ffn2_ready, 1)

            with pe.Fori(0, BATCH) as b:
                pe.wait_ge(xT_loaded, 16 * (b + 1))
                pe.wait_ge(post_done, done(b * NCH))
                v_at = {1: 0, 2: 1, 3: 2, 4: 3}
                for s in range(PRO):
                    pe.wait_ge(q_copied, done(b * STAGES + s))
                    if s < NCH:
                        project(wk_sb, 0, s, q_ready)
                    else:
                        project(wqg_sb, (s - NCH) * P, 0, q_ready)
                    if s in v_at:
                        v_group(v_at[s], b)
                for s in (NCH - 2, NCH - 1):
                    pe.wait_ge(placed[s % 2], 96 * (occurrence(b, s) + 2))
                for j in range(MAXES):
                    row_max(b, 0, 0, j)
                for j in range(4):
                    row_max(b, 0, 1, j)
                pe.wait_ge(q_copied, done(b * STAGES + PRO))
                max_transpose(b, 0, 0)
                for j in range(4, LEAD):
                    row_max(b, 0, 1, j)
                pe.wait_ge(v_copied, done((b + 1) * TILES))
                scores(b, 0, 0)
                attention_steps(pe, step(b))
                pe.wait_ge(gate_copied, done((b + 1) * UNITS))
                denominators(b, NCH - 1, PAIRS - 1)
                with pe.Fori(0, NCH) as c:
                    rest(b, c)

        @block.scalar
        def _(act):
            for s in ACT_SEMS:
                act.sem_inc(s, PRIME)
            act.wait_ge(setup_pe, 1)
            nc.scalar.copy(bv_sb, misc[0:RANK, 0:HID]).then_inc(setup_act, 1)
            act.wait_ge(setup_pe, 3)
            for h in range(HC):
                for q, bank in enumerate(([mx[:, 0, :], mx[:, 1, :]], [ob[:, :], misc[:, :]])[h]):
                    last = nc.scalar.copy(wfcT[:, h, q * CHUNK:(q + 1) * CHUNK], bank)
            last.then_inc(setup_act, 1)
            act.wait_ge(setup_pe, 4)
            for q in range(4):
                last = nc.scalar.copy(wpT[:, 2 * q:2 * q + 2, :], sc[:, q, :].rearrange("p (a c) -> p a c", a=2))
            last.then_inc(setup_act, 1)

            def copy_stage(s_const, b, c=0):
                par, i = s_const % 2, occurrence(b, s_const, c)
                act.wait_ge(q_ready, done(b * STAGES + c * PAIRS + s_const + 1))
                act.wait_ge(low_done[par], done(i))
                nc.scalar.copy(raw[:, par, :], misc[:, :]).then_inc(q_copied, 1)

            def round_stage(s_const, b, c=0):
                par, i = s_const % 2, occurrence(b, s_const, c)
                act.wait_ge(rope_step[par], done(3 * i + 3))
                act.wait_ge(placed[par], 96 * (i + 1))
                nc.scalar.copy(high[:, par, :], raw[:, par, :]).then_inc(rounded[par], 1)

            def copy_v(g, b):
                act.wait_ge(v_ready, done(b * TILES + g + 1))
                nc.scalar.copy(v_sb[:, g * TILES:(g + 1) * TILES, :],
                               sc[:, g, :].rearrange("p (a c) -> p a c", a=TILES)).then_inc(v_copied, 1)

            def copy_o(b, c, p):
                unit = b * UNITS + c * PAIRS + p
                act.wait_ge(pv_done, done((unit + 1) * STEPS))
                act.wait_ge(og_step, done(2 * unit))
                nc.scalar.copy(o_sb[:, :], ob[:, :]).then_inc(o_copied, 1)

            def step(b):
                def emit(c, k):
                    p, t = k // STEPS, k % STEPS
                    unit = b * UNITS + c * PAIRS + p
                    n = (b * UNITS + c * PAIRS) * STEPS + k
                    act.wait_ge(scores_ready, done(n + 1))
                    act.wait_ge(pv_done, done(n + 1 - RING))
                    act.wait_ge(sum_a, done(n + 1 - RING))
                    act.wait_ge(sum_b, done(n + 1 - RING))
                    nc.scalar.activation(probs[:, k % RING, :].rearrange("p (h n) -> p h n", h=2),
                                         sc[:, 2 * (k % 2):2 * (k % 2) + 2, :], ACT.Exp,
                                         scale=float(D) ** -0.5).then_inc(probs_ready, 1)
                    if t == 0 and not first(c, p):
                        copy_o(b, c, p - 1)
                    if t == 5 and has_q(c, p):
                        copy_stage(PRO + p, b, c)
                    if t == 8:
                        act.wait_ge(gate_ready, done(unit + 1))
                        act.wait_ge(og_step, done(2 * unit))
                        nc.scalar.activation(e_sb[:, :], misc[:, :], ACT.Exp, scale=-1.0)
                        nc.scalar.copy(g_sb[:, :], misc[:, :]).then_inc(gate_copied, 1)
                    if t == 10 and has_q(c, p):
                        round_stage(PRO + p, b, c)
                return emit

            def rest(b, c):
                n = b * NCH + c
                act.wait_ge(tr_ready, done(2 * n))
                for h in range(HC):
                    act.wait_ge(attn_ready, done(n * HC + h + 1))
                    nc.scalar.copy(attnT[:, h, :], sc[:, h, :]).then_inc(attn_copied, 1)
                act.wait_ge(var_ready, done(2 * n + 1))
                nc.scalar.activation(std[:, :], var_eps[:, :], ACT.Sqrt).then_inc(std_done, 1)
                for h in range(HC):
                    act.wait_ge(x1t_ready, done(n * HC + h + 1))
                    nc.scalar.copy(x1T[:, h, :], mx[:, h, :]).then_inc(x1t_copied, 1)
                for j in range(JT):
                    act.wait_ge(ffn1_ready, done(n * JT + j + 1))
                    nc.scalar.activation(rr[:, j, :], sc[:, j % 2, :], ACT.Relu).then_inc(relu_done, 1)
                act.wait_ge(var_ready, done(2 * n + 2))
                nc.scalar.activation(std[:, :], var_eps[:, :], ACT.Sqrt).then_inc(std_done, 1)

            with act.Fori(0, BATCH) as b:
                act.wait_ge(post_done, done(b * NCH))
                copy_stage(0, b)
                for s in range(PRO):
                    if s + 1 < PRO:
                        copy_stage(s + 1, b)
                    if s < TILES:
                        copy_v(s, b)
                    round_stage(s, b)
                attention_steps(act, step(b))
                copy_o(b, NCH - 1, PAIRS - 1)
                with act.Fori(0, NCH) as c:
                    rest(b, c)

        @block.gpsimd
        def _(pool):
            for s in POOL_SEMS:
                pool.sem_inc(s, PRIME)

            def gated(b, c, p):
                unit = b * UNITS + c * PAIRS + p
                pool.wait_ge(recip_done, done(unit + 1))
                nc.gpsimd.tensor_tensor(e_sb[:, :], e_sb[:, :], g_sb[:, :], ALU.mult).then_inc(og_step, 1)
                pool.wait_ge(og_step, done(2 * unit + 1))
                pool.wait_ge(o_copied, done(unit + 1))
                nc.gpsimd.tensor_tensor(og[:, c * PAIRS + p, :], o_sb[:, :], e_sb[:, :], ALU.mult)\
                  .then_inc(og_step, 1)

            def step(b):
                def emit(c, k):
                    p, t = k // STEPS, k % STEPS
                    add_exponentials(pool, nc.gpsimd, b, c, k, 0, sum_a)
                    if t == 5 and not first(c, p):
                        gated(b, c, p - 1)
                    if t == 7 and has_q(c, p):
                        rope(nc.gpsimd, PRO + p, b, c)
                    if t == 8 and has_q(c, p):
                        rope_add(nc.gpsimd, PRO + p, b, c)
                    if t == 11 and has_q(c, p):
                        rope_low(nc.gpsimd, PRO + p, b, c)
                return emit

            with pool.Fori(0, BATCH) as b:
                pool.wait_ge(post_done, done(b * NCH))
                for s in range(1, PRO, 2):
                    rope(nc.gpsimd, s, b)
                    rope_add(nc.gpsimd, s, b)
                    rope_low(nc.gpsimd, s, b)
                pool.wait_ge(y_stored, 16 * NCH * b)
                attention_steps(pool, step(b))
                gated(b, NCH - 1, PAIRS - 1)
                with pool.Fori(0, NCH) as c:
                    n = b * NCH + c
                    for j in range(JT):
                        pool.wait_ge(relu_done, done(n * JT + j + 1))
                        nc.gpsimd.tensor_tensor(rr[:, j, :], rr[:, j, :], rr[:, j, :], ALU.mult)\
                          .then_inc(squared, 1)

        @block.vector
        def _(dve):
            for s in DVE_SEMS:
                dve.sem_inc(s, PRIME)

            nc.vector.memset(kb[D:D + 1, :, :].bitcast(F32), 1.0).then_inc(ones_set, 1)
            nc.vector.memset(rot[:, :, :], 0.0).then_inc(ones_set, 1)
            nc.vector.memset(ones[:, :], 1.0).then_inc(ones_set, 1)

            chain = [0]

            def link(ins):
                chain[0] += 1
                ins.then_inc(ln_chain, 1)
                dve.wait_ge(ln_chain, done(chain[0]))

            full, half, neg = scales[:, 0, :], scales[:, 1, :], scales[:, 2, :]
            dve.wait_ge(weights_loaded, 16 * 11)
            nc.vector.tensor_reduce(full[:, 0:JT], wfc_nat, AX_X, ALU.add, apply_absolute_value=True)
            link(nc.vector.tensor_reduce(full[:, JT:JT + HC], wp_nat, AX_X, ALU.add, apply_absolute_value=True))
            nc.vector.tensor_scalar(full[:, 0:JT], full[:, 0:JT], 1.0 / HID, 1e-5, ALU.mult, ALU.max)
            link(nc.vector.tensor_scalar(full[:, JT:JT + HC], full[:, JT:JT + HC], 1.0 / FFN, 1e-5, ALU.mult, ALU.max))
            nc.vector.tensor_scalar(half, full, 0.5, None, ALU.mult)
            link(nc.vector.tensor_scalar(neg, full, -0.5, None, ALU.mult))

            def ternary(dst, w, q):
                nc.vector.tensor_scalar(dst, w, half[:, q:q + 1], full[:, q:q + 1], ALU.is_gt, ALU.mult)
                return nc.vector.tensor_scalar(w, w, neg[:, q:q + 1], full[:, q:q + 1], ALU.is_lt, ALU.mult)

            for j in range(JT):
                last = ternary(wfc_w[:, j, :], wfc_nat[:, j, :], j)
            for h in range(HC):
                last = ternary(wp_w[:, h, :], wp_nat[:, h, :], JT + h)
            link(last)
            link(nc.vector.tensor_tensor(wfc_w, wfc_w, wfc_nat, ALU.subtract))
            dve.wait_ge(setup_pe, 2)
            for j in range(JT):
                last = nc.vector.scalar_tensor_tensor(
                    out=wfc_w[:, j, :], in0=sc[:, j // 2, (j % 2) * HID:(j % 2 + 1) * HID],
                    scalar=gate_sb[:, 0:1], in1=wfc_w[:, j, :], op0=ALU.mult, op1=ALU.add)
            last.then_inc(setup_dve, 1)
            nc.vector.tensor_tensor(wp_w, wp_w, wp_nat, ALU.subtract).then_inc(setup_dve, 1)

            def reduce_max(b, c, p, j):
                unit = b * UNITS + c * PAIRS + p
                if j == 0:
                    dve.wait_ge(max8_done, done(unit - 1))
                dve.wait_ge(max_ready, done(unit * MAXES + j + 1))
                nc.vector.tensor_reduce(maxp[:, p % 2, j:j + 1], mx[:, j % 2, :], AX_X, ALU.max)\
                  .then_inc(maxed, 1)

            def final_max(b, c, p):
                unit = b * UNITS + c * PAIRS + p
                dve.wait_ge(maxed, done((unit + 1) * MAXES))
                dve.wait_ge(mt_ready, done(unit))
                nc.vector.tensor_reduce(max8[:, :], maxp[:, p % 2, :].rearrange("p (q k) -> p q k", k=KEYCH),
                                        AX_X, ALU.max).then_inc(max8_done, 1)

            def copy_max(b, c, p):
                unit = b * UNITS + c * PAIRS + p
                dve.wait_ge(mt_ready, done(unit + 1))
                dve.wait_ge(m_placed, 16 * (unit + 1))
                nc.vector.tensor_scalar(mrow[:, :], misc[0:2 * TILES, 0:P], -1.0, None, ALU.mult)\
                  .then_inc(m_copied, 1)

            def fold_denominator(b, c, p):
                unit = b * UNITS + c * PAIRS + p
                dve.wait_ge(den_ready, done(unit + 1))
                dve.wait_ge(gate_copied, done(unit + 1))
                nc.vector.scalar_tensor_tensor(out=e_sb[:, :], in0=e_sb[:, :], scalar=1.0, in1=misc[:, :],
                                               op0=ALU.add, op1=ALU.mult).then_inc(den_used, 1)

            def reciprocal(b, c, p):
                unit = b * UNITS + c * PAIRS + p
                dve.wait_ge(den_used, done(unit + 1))
                nc.vector.reciprocal(e_sb[:, :], e_sb[:, :]).then_inc(recip_done, 1)

            def step(b):
                def emit(c, k):
                    p, t = k // STEPS, k % STEPS
                    for j in (LEAD + 2 * t, LEAD + 2 * t + 1):
                        ahead = 1 + j // MAXES
                        if exists(c, p, ahead):
                            reduce_max(b, c, p + ahead, j % MAXES)
                            if j == MAXES - 1:
                                final_max(b, c, p + 1)
                    add_exponentials(dve, nc.vector, b, c, k, 1, sum_b)
                    if t == 3 and not first(c, p):
                        fold_denominator(b, c, p - 1)
                    if t == 4 and not first(c, p):
                        reciprocal(b, c, p - 1)
                    if t == 12 and exists(c, p, 1):
                        copy_max(b, c, p + 1)
                return emit

            LN_LINKS = 2 * TILES + 2
            setup_links = chain[0]

            def layer_norm(n, which, src, dst, signal):
                base = setup_links + (2 * n + which) * LN_LINKS
                end = TILES - 1
                nc.vector.bn_stats(stats[:, 0, :], src[:, 0, :]).then_inc(ln_chain, 1)
                for i in range(end):
                    dve.wait_ge(ln_chain, done(base + 2 * i + 1))
                    nc.vector.bn_stats(stats[:, i + 1, :], src[:, i + 1, :]).then_inc(ln_chain, 1)
                    nc.vector.bn_aggr(mv[:, i, :], stats[:, i, :]).then_inc(ln_chain, 1)
                dve.wait_ge(ln_chain, done(base + 2 * end + 1))
                nc.vector.tensor_scalar_add(var_eps[:, 0:end], mv[:, 0:end, 1], EPS).then_inc(ln_chain, 1)
                nc.vector.bn_aggr(mv[:, end, :], stats[:, end, :]).then_inc(ln_chain, 1)
                dve.wait_ge(ln_chain, done(base + 2 * TILES + 1))
                nc.vector.tensor_scalar_add(var_eps[:, end:TILES], mv[:, end:TILES, 1], EPS).then_inc(var_ready, 1)
                dve.wait_ge(std_done, done(2 * n + which + 1))
                nc.vector.reciprocal(rstd[:, :], std[:, :]).then_inc(ln_chain, 1)
                dve.wait_ge(ln_chain, done(base + LN_LINKS))
                for i in range(TILES):
                    last = nc.vector.tensor_scalar(dst[:, i, :], src[:, i, :], mv[:, i, 0:1], rstd[:, i:i + 1],
                                                   ALU.subtract, ALU.mult)
                    if signal is not None:
                        last.then_inc(signal, 1)
                return last

            def rest(b, c):
                n = b * NCH + c
                dve.wait_ge(xres_loaded, 16 * (n + 1))
                for i in range(TILES):
                    if i % 2 == 0:
                        dve.wait_ge(tr_ready, done(2 * n + i // 2 + 1))
                    nc.vector.tensor_tensor(y1[:, i, :], sc[:, 2 + i // 2, (i % 2) * HID:(i % 2 + 1) * HID],
                                            xres[:, i, :], ALU.add).then_inc(res_done, 1)
                dve.wait_ge(res_done, done((n + 1) * TILES))
                layer_norm(n, 0, y1, x1, x1_done)
                for i in range(TILES):
                    if i % 2 == 0:
                        dve.wait_ge(ffn2_ready, done(2 * n + i // 2 + 1))
                    bank = (ob if i < 2 else misc)[:, (i % 2) * HID:(i % 2 + 1) * HID]
                    nc.vector.tensor_tensor(y1[:, i, :], bank, x1[:, i, :], ALU.add).then_inc(y2_done, 1)
                dve.wait_ge(y2_done, done((n + 1) * TILES))
                dve.wait_ge(y_stored, 16 * n)
                layer_norm(n, 1, y1, yout, None).then_inc(post_done, 1)

            with dve.Fori(0, BATCH) as b:
                for s in range(0, PRO, 2):
                    rope(nc.vector, s, b)
                    rope_add(nc.vector, s, b)
                    rope_low(nc.vector, s, b)
                for j in range(MAXES):
                    reduce_max(b, 0, 0, j)
                final_max(b, 0, 0)
                for j in range(LEAD):
                    reduce_max(b, 0, 1, j)
                    if j == 3:
                        copy_max(b, 0, 0)
                dve.wait_ge(y_stored, 16 * NCH * b)
                attention_steps(dve, step(b))
                fold_denominator(b, NCH - 1, PAIRS - 1)
                reciprocal(b, NCH - 1, PAIRS - 1)
                with dve.Fori(0, NCH) as c:
                    rest(b, c)


def has_q(c, p):
    return not (isinstance(c, int) and c == NCH - 1 and p >= 1)


def raw_words(ap):
    return ap.bitcast(F32)


def rotary_tables():
    inv = (np.float32(1) / np.power(10000.0, np.arange(0, ROT, 2) / ROT).astype(np.float32)).astype(np.float32)
    angle = (np.arange(SEQ, dtype=np.float32)[None, :] * inv[:, None]).astype(np.float64)
    cos, sin = np.ones((P, SEQ), np.float32), np.zeros((P, SEQ), np.float32)
    h = ROT // 2
    for base in (0, D):
        cos[base:base + h] = cos[base + h:base + 2 * h] = np.cos(angle)
        sin[base:base + h] = -np.sin(angle)
        sin[base + h:base + 2 * h] = np.sin(angle)
    return cos, sin


def kernel(**inputs):
    import concourse.bacc as _bacc
    from concourse.bass_utils import run_bass_kernel_spmd as _run

    a = {k: np.asarray(v) for k, v in inputs.items()}
    x = a["L0_attn_hidden_states"].reshape(BATCH * SEQ, HID)
    cos, sin = rotary_tables()
    arrays = {
        "x": x, "xT": x.T, "wq": a["L0_attn_Wq"], "wk": a["L0_attn_Wk"], "wv": a["L0_attn_Wv"],
        "wo": a["L0_attn_Wo"], "fast_bT": a["L0_ffn_fast_b"].T, "w_fc": a["L0_ffn_w_fc"],
        "w_proj": a["L0_ffn_w_proj"], "uT": a["L0_ffn_u"].T, "v_lr": a["L0_ffn_v"],
        "gate": np.broadcast_to(a["L0_ffn_gate"].reshape(1, 1), (P, 1)),
        "cos_t": cos, "sin_t": sin, "ident_in": np.eye(P, dtype=np.float32),
    }
    arrays = {k: np.ascontiguousarray(v) for k, v in arrays.items()}
    nc = _bacc.Bacc("TRN2", target_bir_lowering=False, num_devices=1)
    aps = {k: nc.dram_tensor(f"in_{k}", v.shape, mybir.dt.from_np(v.dtype), kind="ExternalInput").ap()
           for k, v in arrays.items()}
    out = nc.dram_tensor("out_y", (BATCH * SEQ, HID), F32, kind="ExternalOutput").ap()
    layer_kernel(nc, out=out, **aps)
    r = _run(nc, [{f"in_{k}": v for k, v in arrays.items()}], core_ids=[0])
    return r.results[0]["out_y"].reshape(BATCH, SEQ, HID)
```

```python
from contextlib import ExitStack

import numpy as np

import concourse.bass as bass
from concourse import mybir

F32 = mybir.dt.float32
F32R = mybir.dt.float32r
ALU = mybir.AluOpType
ACT = mybir.ActivationFunctionType
AX_X = mybir.AxisListType.X

P = 128
BATCH, SEQ, HID = 2, 2048, 256
HEADS, KVH, D = 8, 2, 64
ROT = D // 4
FFN, RANK = 1024, 16
EPS = 1e-5
CHUNK = 512
NCH = SEQ // CHUNK
PAIRS = HEADS // 2
UNITS = NCH * PAIRS
STEPS = SEQ // P
HC = HID // P
KEYCH = SEQ // CHUNK
TILES = CHUNK // P
MAXES = 2 * TILES * KEYCH
JT = FFN // P
STAGES = NCH + UNITS
RING = 4
LEAD = 12
HEAD = 8
PARTS = 4
AHEAD = 3
PRIME = 4


def done(n):
    return n + PRIME


def attention_steps(eng, emit):
    for k in range(HEAD):
        emit(0, k)
    with eng.Fori(0, NCH - 1) as c:
        for k in range(HEAD, HEAD + PAIRS * STEPS):
            emit(c, k)
    for k in range(HEAD, PAIRS * STEPS):
        emit(NCH - 1, k)


def first(c, p):
    return isinstance(c, int) and c == 0 and p == 0


def exists(c, p, ahead):
    return not (isinstance(c, int) and c == NCH - 1 and p + ahead >= PAIRS)


def layer_kernel(nc, x, xT, wq, wk, wv, wo, fast_bT, w_fc, w_proj, uT, v_lr, gate, cos_t, sin_t, ident_in, out):
    ctx = ExitStack()
    with ctx:
        def sb(name, shape, dt=F32):
            return ctx.enter_context(nc.sbuf_tensor(name, shape, dt))

        def ps(name, shape):
            return ctx.enter_context(nc.psum_tensor(name, shape, F32))

        def sem(name):
            return ctx.enter_context(nc.semaphore(name))

        wqg_sb = sb("wqg_sb", [P, HC, 2 * HEADS * D])
        wk_sb = sb("wk_sb", [P, HC, P])
        wv_sb = sb("wv_sb", [P, HC, P])
        wo_sb = sb("wo_sb", [P, PAIRS, HID])
        wfcT = sb("wfcT", [P, HC, FFN])
        wpT = sb("wpT", [P, JT, HID], F32R)
        wp_scale = sb("wp_scale", [P, HID])
        ident = sb("ident", [P, P])
        ones = sb("ones", [P, D])
        gate_sb = sb("gate_sb", [P, 1])
        xT_sb = sb("xT_sb", [P, HC, SEQ])
        ka = sb("ka", [P, KVH, SEQ], F32R)
        kb = sb("kb", [P, KVH, SEQ], F32R)
        v_sb = sb("v_sb", [P, STEPS, P])
        qa = sb("qa", [P, PAIRS, 2, CHUNK], F32R)
        qb = sb("qb", [P, PAIRS, 2, CHUNK], F32R)
        og = sb("og", [P, UNITS, CHUNK])
        cos_sb = sb("cos_sb", [P, 2, CHUNK])
        sin_sb = sb("sin_sb", [P, 2, CHUNK])
        raw = sb("raw", [P, 2, CHUNK])
        rot = sb("rot", [P, 2, CHUNK])
        high = sb("high", [P, 2, CHUNK], F32R)
        low = sb("low", [P, 2, CHUNK], F32R)
        probs = sb("probs", [P, RING, 2 * CHUNK])
        acc = sb("acc", [P, 2, 2 * CHUNK])
        maxp = sb("maxp", [P, 2, MAXES])
        max8 = sb("max8", [P, 2 * TILES])
        mrow = sb("mrow", [2 * TILES, P], F32R)
        oge = sb("oge", [P, 3, CHUNK])
        o_sb, g_sb, e_sb = oge[:, 0, :], oge[:, 1, :], oge[:, 2, :]
        stats = sb("stats", [P, TILES, 6])
        mv = sb("mv", [P, TILES, 2])
        var_eps = sb("var_eps", [P, TILES])
        std = sb("std", [P, TILES])
        rstd = sb("rstd", [P, TILES])
        scales = sb("scales", [P, 3, JT + HC])

        attnT = probs[:, 0, :].rearrange("p (h n) -> p h n", h=HC)
        y1 = probs[:, 1, :].rearrange("p (i c) -> p i c", c=HID)
        x1s = [probs[:, 2 + i, :].rearrange("p (i c) -> p i c", c=HID) for i in range(2)]
        x1T = low[:, :, :].bitcast(F32)
        y2 = oge[:, 0:2, :].rearrange("p a (b c) -> p (a b) c", c=HID)
        xres = acc[:, 0, :].rearrange("p (i c) -> p i c", c=HID)
        yout = acc[:, 1, :].rearrange("p (i c) -> p i c", c=HID)
        relu_ring = [raw[:, 0, :], raw[:, 1, :], high[:, 0, :].bitcast(F32), high[:, 1, :].bitcast(F32)]
        sq_high = qa[:, :, :, :].rearrange("p a h n -> p (a h) n")
        sq_low = qb[:, :, :, :].rearrange("p a h n -> p (a h) n")
        wfc_nat = og[:, 0:4, :].rearrange("p a (b c) -> p (a b) c", c=HID)
        wfc_w = og[:, 4:8, :].rearrange("p a (b c) -> p (a b) c", c=HID)
        wp_nat = og[:, 8:12, :].rearrange("p (a b) c -> p a (b c)", a=HC)
        wp_w = og[:, 12:16, :].rearrange("p (a b) c -> p a (b c)", a=HC)
        uT_sb = probs[0:RANK, 0, :]
        v_lr_sb = probs[0:RANK, 1, 0:HID]
        fbT_sb = probs[0:RANK, 2, 0:RANK]
        bv_sb = probs[0:RANK, 3, 0:HID]

        sc = ps("sc", [P, 4, CHUNK])
        mx = ps("mx", [P, 2, CHUNK])
        ob = ps("ob", [P, CHUNK])
        misc = ps("misc", [P, CHUNK])

        weights_loaded = sem("weights_loaded")
        setup_pe = sem("setup_pe")
        setup_act = sem("setup_act")
        setup_dve = sem("setup_dve")
        ones_set = sem("ones_set")
        xT_loaded = sem("xT_loaded")
        tables_loaded = [sem(f"tables_loaded{i}") for i in range(2)]
        rot_placed = [sem(f"rot_placed{i}") for i in range(2)]
        placed = [sem(f"placed{i}") for i in range(2)]
        m_placed = sem("m_placed")
        xres_loaded = sem("xres_loaded")
        y_stored = sem("y_stored")

        q_ready = sem("q_ready")
        v_ready = sem("v_ready")
        max_ready = sem("max_ready")
        mt_ready = sem("mt_ready")
        scores_ready = sem("scores_ready")
        pv_done = sem("pv_done")
        den_ready = sem("den_ready")
        gate_ready = sem("gate_ready")
        attn_ready = sem("attn_ready")
        tr_ready = sem("tr_ready")
        x1t_ready = sem("x1t_ready")
        ffn1_ready = sem("ffn1_ready")
        ffn2_ready = sem("ffn2_ready")
        PE_SEMS = [q_ready, v_ready, max_ready, mt_ready, scores_ready, pv_done, den_ready, gate_ready,
                   attn_ready, tr_ready, x1t_ready, ffn1_ready, ffn2_ready]

        q_copied = sem("q_copied")
        v_copied = sem("v_copied")
        rounded = [sem(f"rounded{i}") for i in range(2)]
        probs_ready = sem("probs_ready")
        gate_copied = sem("gate_copied")
        o_copied = sem("o_copied")
        attn_copied = sem("attn_copied")
        x1t_copied = sem("x1t_copied")
        relu_done = sem("relu_done")
        std_done = sem("std_done")
        sq_rounded = sem("sq_rounded")
        ACT_SEMS = [q_copied, v_copied, *rounded, probs_ready, gate_copied, o_copied, attn_copied,
                    x1t_copied, relu_done, sq_rounded, std_done]

        maxed = sem("maxed")
        max8_done = sem("max8_done")
        m_copied = sem("m_copied")
        sum_b = sem("sum_b")
        den_used = sem("den_used")
        recip_done = sem("recip_done")
        ln_chain = sem("ln_chain")
        res_done = sem("res_done")
        y2_done = sem("y2_done")
        y2_summed = sem("y2_summed")
        sq_split = sem("sq_split")
        var_ready = sem("var_ready")
        x1_done = sem("x1_done")
        post_done = sem("post_done")
        DVE_SEMS = [maxed, max8_done, m_copied, sum_b, den_used, recip_done, ln_chain, res_done, sq_split, y2_summed,
                    y2_done, var_ready, x1_done, post_done]

        sum_a = sem("sum_a")
        og_step = sem("og_step")
        squared = sem("squared")
        rope_step = [sem(f"rope_step{i}") for i in range(2)]
        low_done = [sem(f"low_done{i}") for i in range(2)]
        POOL_SEMS = [sum_a, og_step, squared, *rope_step, *low_done]

        x_tiles = x.rearrange("(n i p) c -> p n i c", p=P, i=TILES)
        out_tiles = out.rearrange("(n i p) c -> p n i c", p=P, i=TILES)
        xT_v = xT.rearrange("(h p) t -> p h t", p=P)

        def occurrence(b, s_const, c=0):
            return b * (STAGES // 2) + c * (PAIRS // 2) + s_const // 2

        FRONT = [("q", 0)] + [("k", n) for n in range(NCH)] + [("q", u) for u in range(1, AHEAD)]
        PRO = len(FRONT)

        def rope(eng, s_const, b, c=0):
            par, i = s_const % 2, occurrence(b, s_const, c)
            eng.wait_ge(rot_placed[par], 64 * (i + 1))
            eng.wait_ge(tables_loaded[par], 32 * (i + 1))
            eng.tensor_tensor(raw[:, par, :], raw[:, par, :], cos_sb[:, par, :], ALU.mult)\
               .then_inc(rope_step[par], 1)
            eng.tensor_tensor(rot[:, par, :], rot[:, par, :], sin_sb[:, par, :], ALU.mult)\
               .then_inc(rope_step[par], 1)

        def rope_add(eng, s_const, b, c=0):
            par, i = s_const % 2, occurrence(b, s_const, c)
            eng.wait_ge(rope_step[par], done(3 * i + 2))
            eng.tensor_tensor(raw[:, par, :], raw[:, par, :], rot[:, par, :], ALU.add)\
               .then_inc(rope_step[par], 1)

        def rope_low(eng, s_const, b, c=0):
            par, i = s_const % 2, occurrence(b, s_const, c)
            eng.wait_ge(rounded[par], done(i + 1))
            eng.wait_ge(placed[par], 96 * (i + 1))
            eng.tensor_tensor(low[:, par, :], raw[:, par, :], high[:, par, :].bitcast(F32), ALU.subtract)\
               .then_inc(low_done[par], 1)

        def add_exponentials(eng, ops, b, c, k, hd, summed):
            p, t = k // STEPS, k % STEPS
            n = (b * UNITS + c * PAIRS) * STEPS + k
            cols = slice(hd * CHUNK, (hd + 1) * CHUNK)
            total, part = acc[:, p % 2, cols], probs[:, k % RING, cols]
            if t == 1:
                eng.wait_ge(probs_ready, done(n + 1))
                eng.wait_ge(den_ready, done(b * UNITS + c * PAIRS + p - 1))
                ops.tensor_tensor(total, probs[:, (k - 1) % RING, cols], part, ALU.add).then_inc(summed, 2)
            elif t > 1:
                eng.wait_ge(probs_ready, done(n + 1))
                eng.wait_ge(summed, done(n))
                ops.tensor_tensor(total, total, part, ALU.add).then_inc(summed, 1)

        block = ctx.enter_context(nc.Block())

        @block.sync
        def _(sp):
            sp.sem_inc(m_placed, 16)
            sp.sem_inc(y_stored, 16)
            for par in range(2):
                sp.sem_inc(placed[par], 96)
            for dst, src in (
                    (wfc_nat, w_fc.rearrange("(j p) c -> p j c", p=P)),
                    (wp_nat, w_proj.rearrange("(h p) j -> p h j", p=P)),
                    (uT_sb, uT), (v_lr_sb, v_lr), (fbT_sb, fast_bT), (gate_sb[:, :], gate), (ident[:, :], ident_in),
                    (wqg_sb[:, :, :], wq.rearrange("(h p) n -> p h n", p=P)),
                    (wk_sb[:, :, :], wk.rearrange("(h p) n -> p h n", p=P)),
                    (wv_sb[:, :, :], wv.rearrange("(h p) n -> p h n", p=P)),
                    (wo_sb[:, :, :], wo.rearrange("(h p) n -> p h n", p=P))):
                sp.dma_start(dst, src).then_inc(weights_loaded, 16)
            sp.dma_start(xT_sb[:, :, :], xT_v[:, :, 0:SEQ]).then_inc(xT_loaded, 16)

            def tables(s_const, b, chunk, c=0):
                par, i = s_const % 2, occurrence(b, s_const, c)
                sp.wait_ge(low_done[par], done(i))
                for dst, src in ((cos_sb, cos_t), (sin_sb, sin_t)):
                    sp.dma_start(dst[:, par, :], src[:, bass.ds(chunk * CHUNK, CHUNK)])\
                      .then_inc(tables_loaded[par], 16)

            def swap_rows(s_const, b, c=0):
                par, h = s_const % 2, ROT // 2
                sp.wait_ge(q_copied, done(b * STAGES + c * PAIRS + s_const + 1))
                for base in (0, D):
                    for to, frm in ((base, base + h), (base + h, base)):
                        sp.dma_start(rot[to:to + h, par, :], raw[frm:frm + h, par, :])\
                          .then_inc(rot_placed[par], 16)

            def place(s_const, b, targets, c=0):
                par, i = s_const % 2, occurrence(b, s_const, c)
                sp.wait_ge(low_done[par], done(i + 1))
                for part, hd, dst in targets:
                    sp.dma_start(raw_words(dst), raw_words(part[hd * D:(hd + 1) * D, par, :]))\
                      .then_inc(placed[par], 16)

            def k_targets(n):
                keys = slice(n * CHUNK, (n + 1) * CHUNK)
                return [t for g in range(KVH) for t in (
                    (high, g, ka[0:D, g, keys]), (low, g, ka[D:P, g, keys]), (high, g, kb[0:D, g, keys]))]

            def q_targets(slot):
                return [t for hd in range(2) for t in (
                    (high, hd, qa[0:D, slot, hd, :]), (high, hd, qa[D:P, slot, hd, :]), (low, hd, qb[0:D, slot, hd, :]))]

            def place_max(b, c, p):
                sp.wait_ge(m_copied, done(b * UNITS + c * PAIRS + p + 1))
                sp.dma_start(raw_words(qb[D:D + 1, p % PAIRS, :, :]), raw_words(mrow[:, :])).then_inc(m_placed, 16)

            def step(b):
                def emit(c, k):
                    p, t = k // STEPS, k % STEPS
                    unit = b * UNITS + c * PAIRS + p
                    s_const = NCH + AHEAD + p
                    if t == 2 and has_q(c, p):
                        tables(s_const, b, c + (p + AHEAD) // PAIRS, c)
                    if t == 6 and has_q(c, p):
                        swap_rows(s_const, b, c)
                    if t == 14 and has_q(c, p):
                        place(s_const, b, q_targets((p + AHEAD) % PAIRS), c)
                    if t == 13 and exists(c, p, 1):
                        place_max(b, c, p + 1)
                return emit

            with sp.Fori(0, BATCH) as b:
                sp.wait_ge(ones_set, 3)
                sp.wait_ge(post_done, done(b * NCH))
                chunk_of = [n if what == "k" else 0 for what, n in FRONT]
                tables(0, b, 0)
                tables(1, b, 0)
                swap_rows(0, b)
                for s, (what, n) in enumerate(FRONT):
                    if s + 1 < PRO:
                        swap_rows(s + 1, b)
                    place(s, b, k_targets(n) if what == "k" else q_targets(n))
                    if s + 2 < PRO:
                        tables(s + 2, b, chunk_of[s + 2])
                place_max(b, 0, 0)
                attention_steps(sp, step(b))

                def load_residual(c):
                    n = b * NCH + c
                    if c == 0:
                        sp.wait_ge(og_step, done(2 * UNITS * (b + 1)))
                    sp.wait_ge(res_done, done(n * TILES))
                    sp.dma_start(xres, x_tiles[:, n, :, :]).then_inc(xres_loaded, 16)

                load_residual(0)
                with sp.If(b < BATCH - 1):
                    sp.wait_ge(gate_ready, done((b + 1) * UNITS))
                    sp.dma_start(xT_sb[:, :, :], xT_v[:, :, SEQ:2 * SEQ]).then_inc(xT_loaded, 16)
                load_residual(1)
                for c in range(NCH):
                    n = b * NCH + c
                    sp.wait_ge(post_done, done(n + 1))
                    sp.dma_start(out_tiles[:, n, :, :], yout).then_inc(y_stored, 16)
                    if c + 2 < NCH:
                        load_residual(c + 2)
            sp.wait_ge(y_stored, 16 * (BATCH * NCH + 1))

        @block.tensor
        def _(pe):
            for s in PE_SEMS:
                pe.sem_inc(s, PRIME)

            pe.wait_ge(weights_loaded, 16 * 11)
            nc.tensor.matmul(misc[0:RANK, 0:HID], fbT_sb, v_lr_sb, start=True, stop=True).then_inc(setup_pe, 1)
            pe.wait_ge(setup_act, 1)
            for j in range(JT):
                mm = nc.tensor.matmul(sc[:, j // 2, (j % 2) * HID:(j % 2 + 1) * HID],
                                      uT_sb[:, j * P:(j + 1) * P], bv_sb, start=True, stop=True)
            mm.then_inc(setup_pe, 1)
            pe.wait_ge(setup_dve, 1)
            banks = [mx[:, 0, :], mx[:, 1, :], ob[:, :], misc[:, :]]
            for h in range(HC):
                for j in range(JT):
                    tr = nc.tensor.transpose(banks[2 * h + j // 4][:, (j % 4) * P:(j % 4 + 1) * P],
                                             wfc_w[:, j, h * P:(h + 1) * P], ident[:, :])
            tr.then_inc(setup_pe, 1)
            pe.wait_ge(setup_dve, 2)
            for j in range(JT):
                for h in range(HC):
                    tr = nc.tensor.transpose(sc[:, j // 2, (j % 2) * HID + h * P:(j % 2) * HID + (h + 1) * P],
                                             wp_w[:, h, j * P:(j + 1) * P], ident[:, :])
            pe.wait_ge(setup_act, 2)
            pe.wait_ge(ones_set, 3)
            for i in range(2):
                mm = nc.tensor.matmul(misc[i * D:(i + 1) * D, 0:HID], ones[:, :], acc[:, 0, 0:HID],
                                      start=True, stop=True)
            mm.then_inc(setup_pe, 1)
            pe.wait_ge(setup_act, 3)

            def project(w, col, chunk, semaphore):
                for h in range(HC):
                    mm = nc.tensor.matmul(misc[:, :], w[:, h, col:col + P],
                                          xT_sb[:, h, bass.ds(chunk * CHUNK, CHUNK)],
                                          start=(h == 0), stop=(h == HC - 1))
                mm.then_inc(semaphore, 1)

            def v_group(g, b):
                for i in range(TILES):
                    tile = g * TILES + i
                    for h in range(HC):
                        mm = nc.tensor.matmul(sc[:, g, i * P:(i + 1) * P], xT_sb[:, h, tile * P:(tile + 1) * P],
                                              wv_sb[:, h, :], start=(h == 0), stop=(h == HC - 1))
                mm.then_inc(v_ready, 1)

            def row_max(b, c, p, j):
                kc, hd, st = j // (2 * TILES), j // TILES % 2, j % TILES
                unit = b * UNITS + c * PAIRS + p
                if j == 0 and not first(c, p):
                    s = NCH + p
                    pe.wait_ge(placed[s % 2], 96 * (occurrence(b, s, c) + 2))
                pe.wait_ge(maxed, done(unit * MAXES + j - 1))
                nc.tensor.matmul(mx[:, j % 2, :], qa[:, p % PAIRS, hd, st * P:(st + 1) * P],
                                 ka[:, p % PAIRS // 2, kc * CHUNK:(kc + 1) * CHUNK],
                                 start=True, stop=True).then_inc(max_ready, 1)

            def max_transpose(b, c, p):
                pe.wait_ge(max8_done, done(b * UNITS + c * PAIRS + p + 1))
                nc.tensor.transpose(misc[0:2 * TILES, 0:P], max8[:, :], ident[:, :]).then_inc(mt_ready, 1)

            def scores(b, c, k):
                p, t = k // STEPS, k % STEPS
                n = (b * UNITS + c * PAIRS) * STEPS + k
                keys, kv = slice(t * P, (t + 1) * P), p % PAIRS // 2
                if t == 0:
                    pe.wait_ge(m_placed, 16 * (b * UNITS + c * PAIRS + p + 2))
                pe.wait_ge(probs_ready, done(n - 1))
                for hd in range(2):
                    nc.tensor.matmul(sc[:, 2 * (k % 2) + hd, :], ka[:, kv, keys], qa[:, p % PAIRS, hd, :],
                                     start=True, stop=False)
                for hd in range(2):
                    mm = nc.tensor.matmul(sc[:, 2 * (k % 2) + hd, :], kb[0:D + 1, kv, keys],
                                          qb[0:D + 1, p % PAIRS, hd, :], start=False, stop=True)
                mm.then_inc(scores_ready, 1)

            def weighted_v(b, c, k):
                p, t = k // STEPS, k % STEPS
                n = (b * UNITS + c * PAIRS) * STEPS + k
                kv = p % PAIRS // 2
                pe.wait_ge(probs_ready, done(n + 1))
                if t == 0:
                    pe.wait_ge(o_copied, done(b * UNITS + c * PAIRS + p))
                for hd in range(2):
                    mm = nc.tensor.matmul(ob[hd * D:(hd + 1) * D, :], v_sb[:, t, kv * D:(kv + 1) * D],
                                          probs[:, k % RING, hd * CHUNK:(hd + 1) * CHUNK],
                                          start=(t == 0), stop=(t == STEPS - 1))
                mm.then_inc(pv_done, 1)

            def denominators(b, c, p):
                unit = b * UNITS + c * PAIRS + p
                pe.wait_ge(sum_a, done((unit + 1) * STEPS))
                pe.wait_ge(sum_b, done((unit + 1) * STEPS))
                for hd in range(2):
                    mm = nc.tensor.matmul(misc[hd * D:(hd + 1) * D, :], ones[:, :],
                                          acc[:, p % 2, hd * CHUNK:(hd + 1) * CHUNK], start=True, stop=True)
                mm.then_inc(den_ready, 1)

            def step(b):
                def emit(c, k):
                    p, t = k // STEPS, k % STEPS
                    unit = b * UNITS + c * PAIRS + p

                    def look_ahead(j):
                        ahead = 1 + j // MAXES
                        if exists(c, p, ahead):
                            row_max(b, c, p + ahead, j % MAXES)

                    if not (isinstance(c, int) and c == NCH - 1 and k == PAIRS * STEPS - 1):
                        scores(b, c, k + 1)
                    look_ahead(LEAD + 2 * t)
                    if t % 2 == 0:
                        look_ahead(LEAD + 2 * t + 1)
                    if t % 2:
                        weighted_v(b, c, k - 1)
                        weighted_v(b, c, k)
                    if t == 1 and not first(c, p):
                        pe.wait_ge(m_copied, done(unit + 1))
                        denominators(b, c, p - 1)
                    if t == 5 and has_q(c, p):
                        if first(c, p):
                            pe.wait_ge(m_copied, done(unit + 1))
                        else:
                            pe.wait_ge(den_used, done(unit))
                        project(wqg_sb, (p + AHEAD) % PAIRS * P, c + (p + AHEAD) // PAIRS, q_ready)
                    if t == 9:
                        if has_q(c, p):
                            pe.wait_ge(q_copied, done(b * STAGES + c * PAIRS + PRO + p + 1))
                        else:
                            pe.wait_ge(den_used, done(unit))
                        project(wqg_sb, HEADS * D + p % PAIRS * P, c, gate_ready)
                    if t == 11 and exists(c, p, 1):
                        pe.wait_ge(gate_copied, done(unit + 1))
                        max_transpose(b, c, p + 1)
                    if t % 2:
                        look_ahead(LEAD + 2 * t + 1)
                return emit

            def output_projection(n, c):
                pe.wait_ge(attn_copied, done(n * HC))
                for h in range(HC):
                    for p in range(PAIRS):
                        mm = nc.tensor.matmul(sc[:, h, :], wo_sb[:, p, h * P:(h + 1) * P],
                                              og[:, c * PAIRS + p, :], start=(p == 0), stop=(p == PAIRS - 1))
                    mm.then_inc(attn_ready, 1)

            def output_transposes(n):
                pe.wait_ge(attn_copied, done((n + 1) * HC))
                pe.wait_ge(res_done, done(n * TILES))
                for i in range(TILES):
                    for h in range(HC):
                        tr = nc.tensor.transpose(sc[:, 2 + i // 2, (i % 2) * HID + h * P:(i % 2) * HID + (h + 1) * P],
                                                 attnT[:, h, i * P:(i + 1) * P], ident[:, :])
                    if i % 2:
                        tr.then_inc(tr_ready, 1)

            def x1_transposes(n, x1):
                pe.wait_ge(x1_done, done((n + 1) * TILES))
                pe.wait_ge(relu_done, done(n * JT))
                for h in range(HC):
                    for i in range(TILES):
                        tr = nc.tensor.transpose(mx[:, h, i * P:(i + 1) * P], x1[:, i, h * P:(h + 1) * P], ident[:, :])
                    tr.then_inc(x1t_ready, 1)

            def ffn_up(n):
                pe.wait_ge(x1t_copied, done((n + 1) * HC))
                for j in range(JT):
                    if j >= 2:
                        pe.wait_ge(relu_done, done(n * JT + j - 1))
                    for h in range(HC):
                        mm = nc.tensor.matmul(mx[:, j % 2, :], wfcT[:, h, j * P:(j + 1) * P], x1T[:, h, :],
                                              start=(h == 0), stop=(h == HC - 1))
                    mm.then_inc(ffn1_ready, 1)

            def ffn_down(n):
                pe.wait_ge(sq_split, done((n + 1) * JT))
                pe.wait_ge(y2_done, done(n * TILES))
                for i in range(TILES):
                    bank = (ob if i < 2 else misc)[:, (i % 2) * HID:(i % 2 + 1) * HID]
                    for j in range(JT):
                        for part in (sq_high, sq_low):
                            mm = nc.tensor.matmul(bank, part[:, j, i * P:(i + 1) * P], wpT[:, j, :],
                                                  start=(j == 0 and part is sq_high),
                                                  stop=(j == JT - 1 and part is sq_low))
                    if i % 2:
                        mm.then_inc(ffn2_ready, 1)

            with pe.Fori(0, BATCH) as b:
                pe.wait_ge(xT_loaded, 16 * (b + 1))
                pe.wait_ge(post_done, done(b * NCH))
                for s, (what, n) in enumerate(FRONT):
                    pe.wait_ge(q_copied, done(b * STAGES + s))
                    if what == "k":
                        project(wk_sb, 0, n, q_ready)
                    else:
                        project(wqg_sb, n * P, 0, q_ready)
                    if s in (1, 2, 3, 4):
                        v_group(s - 1, b)
                for n in range(KEYCH):
                    s = FRONT.index(("k", n))
                    if n == 0:
                        pe.wait_ge(placed[0], 96 * (occurrence(b, 0) + 2))
                    pe.wait_ge(placed[s % 2], 96 * (occurrence(b, s) + 2))
                    for j in range(2 * TILES * n, 2 * TILES * (n + 1)):
                        row_max(b, 0, 0, j)
                for j in range(4):
                    row_max(b, 0, 1, j)
                pe.wait_ge(q_copied, done(b * STAGES + PRO))
                max_transpose(b, 0, 0)
                for j in range(4, LEAD):
                    row_max(b, 0, 1, j)
                pe.wait_ge(v_copied, done((b + 1) * TILES))
                scores(b, 0, 0)
                attention_steps(pe, step(b))
                pe.wait_ge(gate_copied, done((b + 1) * UNITS))
                denominators(b, NCH - 1, PAIRS - 1)
                first_n = b * NCH
                output_projection(first_n, 0)
                output_transposes(first_n)
                output_projection(first_n + 1, 1)
                for c in range(NCH):
                    x1_transposes(first_n + c, x1s[c % 2])
                    ffn_up(first_n + c)
                    if c + 1 < NCH:
                        output_transposes(first_n + c + 1)
                    if c + 2 < NCH:
                        if c + 2 == NCH - 1:
                            pe.wait_ge(og_step, done(2 * UNITS * (b + 1)))
                        output_projection(first_n + c + 2, c + 2)
                    ffn_down(first_n + c)

        @block.scalar
        def _(act):
            for s in ACT_SEMS:
                act.sem_inc(s, PRIME)
            act.wait_ge(setup_pe, 1)
            nc.scalar.copy(bv_sb, misc[0:RANK, 0:HID]).then_inc(setup_act, 1)
            act.wait_ge(setup_pe, 3)
            for h in range(HC):
                for q, bank in enumerate(([mx[:, 0, :], mx[:, 1, :]], [ob[:, :], misc[:, :]])[h]):
                    last = nc.scalar.copy(wfcT[:, h, q * CHUNK:(q + 1) * CHUNK], bank)
            last.then_inc(setup_act, 1)
            act.wait_ge(setup_pe, 4)
            for q in range(4):
                nc.scalar.copy(wpT[:, 2 * q:2 * q + 2, :], sc[:, q, :].rearrange("p (a c) -> p a c", a=2))
            last = nc.scalar.copy(wp_scale[:, :], misc[:, 0:HID])
            last.then_inc(setup_act, 1)

            def copy_stage(s_const, b, c=0):
                par, i = s_const % 2, occurrence(b, s_const, c)
                act.wait_ge(q_ready, done(b * STAGES + c * PAIRS + s_const + 1))
                act.wait_ge(low_done[par], done(i))
                nc.scalar.copy(raw[:, par, :], misc[:, :]).then_inc(q_copied, 1)

            def round_stage(s_const, b, c=0):
                par, i = s_const % 2, occurrence(b, s_const, c)
                act.wait_ge(rope_step[par], done(3 * i + 3))
                act.wait_ge(placed[par], 96 * (i + 1))
                nc.scalar.copy(high[:, par, :], raw[:, par, :]).then_inc(rounded[par], 1)

            def copy_v(g, b):
                act.wait_ge(v_ready, done(b * TILES + g + 1))
                nc.scalar.copy(v_sb[:, g * TILES:(g + 1) * TILES, :],
                               sc[:, g, :].rearrange("p (a c) -> p a c", a=TILES)).then_inc(v_copied, 1)

            def copy_o(b, c, p):
                unit = b * UNITS + c * PAIRS + p
                act.wait_ge(pv_done, done((unit + 1) * STEPS))
                act.wait_ge(og_step, done(2 * unit))
                nc.scalar.copy(o_sb, ob[:, :]).then_inc(o_copied, 1)

            def step(b):
                def emit(c, k):
                    p, t = k // STEPS, k % STEPS
                    unit = b * UNITS + c * PAIRS + p
                    n = (b * UNITS + c * PAIRS) * STEPS + k
                    act.wait_ge(scores_ready, done(n + 1))
                    act.wait_ge(pv_done, done(n + 1 - RING))
                    act.wait_ge(sum_a, done(n + 1 - RING))
                    act.wait_ge(sum_b, done(n + 1 - RING))
                    nc.scalar.activation(probs[:, k % RING, :].rearrange("p (h n) -> p h n", h=2),
                                         sc[:, 2 * (k % 2):2 * (k % 2) + 2, :], ACT.Exp,
                                         scale=float(D) ** -0.5).then_inc(probs_ready, 1)
                    if t == 0 and not first(c, p):
                        copy_o(b, c, p - 1)
                    if t == 6 and has_q(c, p):
                        copy_stage(PRO + p, b, c)
                    if t == 10:
                        act.wait_ge(gate_ready, done(unit + 1))
                        act.wait_ge(og_step, done(2 * unit))
                        nc.scalar.activation(e_sb, misc[:, :], ACT.Exp, scale=-1.0)
                        nc.scalar.copy(g_sb, misc[:, :]).then_inc(gate_copied, 1)
                    if t == 11 and has_q(c, p):
                        round_stage(PRO + p, b, c)
                return emit

            def copy_attention(n):
                act.wait_ge(tr_ready, done(2 * n))
                for h in range(HC):
                    act.wait_ge(attn_ready, done(n * HC + h + 1))
                    nc.scalar.copy(attnT[:, h, :], sc[:, h, :]).then_inc(attn_copied, 1)

            def deviation(count):
                act.wait_ge(var_ready, done(count + 1))
                nc.scalar.activation(std[:, :], var_eps[:, :], ACT.Sqrt).then_inc(std_done, 1)

            def copy_x1(n):
                act.wait_ge(ffn1_ready, done(n * JT))
                for h in range(HC):
                    act.wait_ge(x1t_ready, done(n * HC + h + 1))
                    nc.scalar.copy(x1T[:, h, :], mx[:, h, :]).then_inc(x1t_copied, 1)

            def relu(n, j):
                act.wait_ge(sq_split, done(n * JT + j + 1 - len(relu_ring)))
                act.wait_ge(ffn1_ready, done(n * JT + j + 1))
                nc.scalar.activation(relu_ring[j % 4], mx[:, j % 2, :], ACT.Relu).then_inc(relu_done, 1)

            def round_square(n, j):
                if j == 0:
                    act.wait_ge(ffn2_ready, done(2 * n))
                act.wait_ge(squared, done(n * JT + j + 1))
                nc.scalar.copy(sq_high[:, j, :], relu_ring[j % 4]).then_inc(sq_rounded, 1)

            with act.Fori(0, BATCH) as b:
                act.wait_ge(post_done, done(b * NCH))
                copy_stage(0, b)
                for s in range(PRO):
                    if s + 1 < PRO:
                        copy_stage(s + 1, b)
                    if 1 <= s + 1 <= TILES:
                        copy_v(s, b)
                    round_stage(s, b)
                attention_steps(act, step(b))
                copy_o(b, NCH - 1, PAIRS - 1)
                copy_attention(b * NCH)
                deviation(2 * b * NCH)
                copy_attention(b * NCH + 1)
                for c in range(NCH):
                    n = b * NCH + c
                    copy_x1(n)
                    for j in range(JT + 1):
                        if j < JT:
                            relu(n, j)
                        if j >= 1:
                            round_square(n, j - 1)
                        if j == JT // 2 and c >= 1:
                            deviation(2 * n)
                    if c + 1 < NCH:
                        deviation(2 * n + 1)
                    if c + 2 < NCH:
                        copy_attention(n + 2)
                deviation(2 * (b + 1) * NCH - 1)

        @block.gpsimd
        def _(pool):
            for s in POOL_SEMS:
                pool.sem_inc(s, PRIME)

            def gated(b, c, p):
                unit = b * UNITS + c * PAIRS + p
                pool.wait_ge(recip_done, done(PARTS * (unit + 1)))
                nc.gpsimd.tensor_tensor(e_sb, e_sb, g_sb, ALU.mult).then_inc(og_step, 1)
                pool.wait_ge(og_step, done(2 * unit + 1))
                pool.wait_ge(o_copied, done(unit + 1))
                nc.gpsimd.tensor_tensor(og[:, c * PAIRS + p, :], o_sb, e_sb, ALU.mult)\
                  .then_inc(og_step, 1)

            def step(b):
                def emit(c, k):
                    p, t = k // STEPS, k % STEPS
                    add_exponentials(pool, nc.gpsimd, b, c, k, 0, sum_a)
                    if t == 7 and not first(c, p):
                        gated(b, c, p - 1)
                    if t == 8 and has_q(c, p):
                        rope(nc.gpsimd, PRO + p, b, c)
                    if t == 9 and has_q(c, p):
                        rope_add(nc.gpsimd, PRO + p, b, c)
                    if t == 12 and has_q(c, p):
                        rope_low(nc.gpsimd, PRO + p, b, c)
                return emit

            with pool.Fori(0, BATCH) as b:
                pool.wait_ge(post_done, done(b * NCH))
                for s in range(2, PRO):
                    rope(nc.gpsimd, s, b)
                    rope_add(nc.gpsimd, s, b)
                    rope_low(nc.gpsimd, s, b)
                pool.wait_ge(y_stored, 16 * (NCH * b + 1))
                attention_steps(pool, step(b))
                gated(b, NCH - 1, PAIRS - 1)
                with pool.Fori(0, NCH) as c:
                    n = b * NCH + c
                    for j in range(JT):
                        pool.wait_ge(relu_done, done(n * JT + j + 1))
                        square = relu_ring[j % 4]
                        nc.gpsimd.tensor_tensor(square, square, square, ALU.mult).then_inc(squared, 1)

        @block.vector
        def _(dve):
            for s in DVE_SEMS:
                dve.sem_inc(s, PRIME)

            nc.vector.memset(kb[D:D + 1, :, :].bitcast(F32), 1.0).then_inc(ones_set, 1)
            nc.vector.memset(rot[:, :, :], 0.0).then_inc(ones_set, 1)
            nc.vector.memset(ones[:, :], 1.0).then_inc(ones_set, 1)

            chain = [0]

            def link(ins):
                chain[0] += 1
                ins.then_inc(ln_chain, 1)
                dve.wait_ge(ln_chain, done(chain[0]))

            full, half, neg = scales[:, 0, :], scales[:, 1, :], scales[:, 2, :]
            dve.wait_ge(weights_loaded, 16 * 11)
            nc.vector.tensor_reduce(full[:, 0:JT], wfc_nat, AX_X, ALU.add, apply_absolute_value=True)
            link(nc.vector.tensor_reduce(full[:, JT:JT + HC], wp_nat, AX_X, ALU.add, apply_absolute_value=True))
            nc.vector.tensor_scalar(full[:, 0:JT], full[:, 0:JT], 1.0 / HID, 1e-5, ALU.mult, ALU.max)
            link(nc.vector.tensor_scalar(full[:, JT:JT + HC], full[:, JT:JT + HC], 1.0 / FFN, 1e-5, ALU.mult, ALU.max))
            nc.vector.tensor_scalar(half, full, 0.5, None, ALU.mult)
            link(nc.vector.tensor_scalar(neg, full, -0.5, None, ALU.mult))

            def ternary(dst, w, q):
                times = (full[:, q:q + 1], ALU.mult) if q < JT else (None, ALU.bypass)
                nc.vector.tensor_scalar(dst, w, half[:, q:q + 1], times[0], ALU.is_gt, times[1])
                return nc.vector.tensor_scalar(w, w, neg[:, q:q + 1], times[0], ALU.is_lt, times[1])

            for j in range(JT):
                last = ternary(wfc_w[:, j, :], wfc_nat[:, j, :], j)
            for h in range(HC):
                last = ternary(wp_w[:, h, :], wp_nat[:, h, :], JT + h)
                last = nc.vector.tensor_scalar(acc[:, 0, h * P:(h + 1) * P], ident[:, :],
                                               full[:, JT + h:JT + h + 1], None, ALU.mult)
            link(last)
            link(nc.vector.tensor_tensor(wfc_w, wfc_w, wfc_nat, ALU.subtract))
            dve.wait_ge(setup_pe, 2)
            for j in range(JT):
                last = nc.vector.scalar_tensor_tensor(
                    out=wfc_w[:, j, :], in0=sc[:, j // 2, (j % 2) * HID:(j % 2 + 1) * HID],
                    scalar=gate_sb[:, 0:1], in1=wfc_w[:, j, :], op0=ALU.mult, op1=ALU.add)
            last.then_inc(setup_dve, 1)
            nc.vector.tensor_tensor(wp_w, wp_w, wp_nat, ALU.subtract).then_inc(setup_dve, 1)

            def reduce_max(b, c, p, j):
                unit = b * UNITS + c * PAIRS + p
                if j == 0:
                    dve.wait_ge(max8_done, done(unit - 1))
                dve.wait_ge(max_ready, done(unit * MAXES + j + 1))
                column = j % (2 * TILES) * KEYCH + j // (2 * TILES)
                nc.vector.tensor_reduce(maxp[:, p % 2, column:column + 1], mx[:, j % 2, :], AX_X, ALU.max)\
                  .then_inc(maxed, 1)

            def final_max(b, c, p):
                unit = b * UNITS + c * PAIRS + p
                dve.wait_ge(maxed, done((unit + 1) * MAXES))
                dve.wait_ge(mt_ready, done(unit))
                nc.vector.tensor_reduce(max8[:, :], maxp[:, p % 2, :].rearrange("p (q k) -> p q k", k=KEYCH),
                                        AX_X, ALU.max).then_inc(max8_done, 1)

            def copy_max(b, c, p):
                unit = b * UNITS + c * PAIRS + p
                dve.wait_ge(mt_ready, done(unit + 1))
                dve.wait_ge(m_placed, 16 * (unit + 1))
                nc.vector.tensor_scalar(mrow[:, :], misc[0:2 * TILES, 0:P], -1.0, None, ALU.mult)\
                  .then_inc(m_copied, 1)

            def fold_denominator(b, c, p):
                unit = b * UNITS + c * PAIRS + p
                dve.wait_ge(den_ready, done(unit + 1))
                dve.wait_ge(gate_copied, done(unit + 1))
                nc.vector.scalar_tensor_tensor(out=e_sb, in0=e_sb, scalar=1.0, in1=misc[:, :],
                                               op0=ALU.add, op1=ALU.mult).then_inc(den_used, 1)

            def reciprocal(b, c, p, q):
                unit, cols = b * UNITS + c * PAIRS + p, slice(q * CHUNK // PARTS, (q + 1) * CHUNK // PARTS)
                if q == 0:
                    dve.wait_ge(den_used, done(unit + 1))
                nc.vector.reciprocal(e_sb[:, cols], e_sb[:, cols]).then_inc(recip_done, 1)

            def step(b):
                def emit(c, k):
                    p, t = k // STEPS, k % STEPS

                    def look_ahead(j):
                        ahead = 1 + j // MAXES
                        if exists(c, p, ahead):
                            reduce_max(b, c, p + ahead, j % MAXES)
                            if j == MAXES - 1:
                                final_max(b, c, p + 1)

                    look_ahead(LEAD + 2 * t)
                    if t % 2 == 0:
                        look_ahead(LEAD + 2 * t + 1)
                    add_exponentials(dve, nc.vector, b, c, k, 1, sum_b)
                    if t % 2:
                        look_ahead(LEAD + 2 * t + 1)
                    if t == 2 and not first(c, p):
                        fold_denominator(b, c, p - 1)
                    if 3 <= t < 3 + PARTS and not first(c, p):
                        reciprocal(b, c, p - 1, t - 3)
                    if t == 12 and exists(c, p, 1):
                        copy_max(b, c, p + 1)
                return emit

            LN_LINKS = 2 * TILES + 2
            setup_links = chain[0]

            def variances(count, src):
                base = setup_links + count * LN_LINKS
                end = TILES - 1
                nc.vector.bn_stats(stats[:, 0, :], src[:, 0, :]).then_inc(ln_chain, 1)
                for i in range(end):
                    dve.wait_ge(ln_chain, done(base + 2 * i + 1))
                    nc.vector.bn_stats(stats[:, i + 1, :], src[:, i + 1, :]).then_inc(ln_chain, 1)
                    nc.vector.bn_aggr(mv[:, i, :], stats[:, i, :]).then_inc(ln_chain, 1)
                dve.wait_ge(ln_chain, done(base + 2 * end + 1))
                nc.vector.tensor_scalar_add(var_eps[:, 0:end], mv[:, 0:end, 1], EPS).then_inc(ln_chain, 1)
                nc.vector.bn_aggr(mv[:, end, :], stats[:, end, :]).then_inc(ln_chain, 1)
                dve.wait_ge(ln_chain, done(base + 2 * TILES + 1))
                nc.vector.tensor_scalar_add(var_eps[:, end:TILES], mv[:, end:TILES, 1], EPS).then_inc(var_ready, 1)

            def normalise(count, src, dst, signal):
                dve.wait_ge(std_done, done(count + 1))
                nc.vector.reciprocal(rstd[:, :], std[:, :]).then_inc(ln_chain, 1)
                dve.wait_ge(ln_chain, done(setup_links + (count + 1) * LN_LINKS))
                for i in range(TILES):
                    last = nc.vector.tensor_scalar(dst[:, i, :], src[:, i, :], mv[:, i, 0:1], rstd[:, i:i + 1],
                                                   ALU.subtract, ALU.mult)
                    if signal is not None:
                        last.then_inc(signal, 1)
                return last

            def first_norm(n, c, count):
                dve.wait_ge(xres_loaded, 16 * (n + 1))
                for i in range(TILES):
                    if i % 2 == 0:
                        dve.wait_ge(tr_ready, done(2 * n + i // 2 + 1))
                    nc.vector.tensor_tensor(y1[:, i, :], sc[:, 2 + i // 2, (i % 2) * HID:(i % 2 + 1) * HID],
                                            xres[:, i, :], ALU.add).then_inc(res_done, 1)
                dve.wait_ge(res_done, done((n + 1) * TILES))
                variances(count, y1)
                normalise(count, y1, x1s[c % 2], x1_done)

            def second_sum(n, c, count):
                for i in range(TILES):
                    if i % 2 == 0:
                        dve.wait_ge(ffn2_ready, done(2 * n + i // 2 + 1))
                    bank = (ob if i < 2 else misc)[:, (i % 2) * HID:(i % 2 + 1) * HID]
                    nc.vector.tensor_tensor(y2[:, i, :], bank, wp_scale[:, :], ALU.mult).then_inc(y2_done, 1)
                for i in range(TILES):
                    dve.wait_ge(y2_done, done(n * TILES + i + 1))
                    last = nc.vector.tensor_tensor(y2[:, i, :], y2[:, i, :], x1s[c % 2][:, i, :], ALU.add)
                last.then_inc(y2_summed, 1)
                dve.wait_ge(y2_summed, done(n + 1))
                variances(count, y2)

            def second_norm(n, count):
                dve.wait_ge(y_stored, 16 * (n + 1))
                normalise(count, y2, yout, None).then_inc(post_done, 1)

            def split_square(n, j):
                dve.wait_ge(sq_rounded, done(n * JT + j + 1))
                nc.vector.tensor_tensor(sq_low[:, j, :], relu_ring[j % 4], sq_high[:, j, :].bitcast(F32),
                                        ALU.subtract).then_inc(sq_split, 1)

            with dve.Fori(0, BATCH) as b:
                for s in range(2):
                    rope(nc.vector, s, b)
                    rope_add(nc.vector, s, b)
                    rope_low(nc.vector, s, b)
                for j in range(MAXES):
                    reduce_max(b, 0, 0, j)
                final_max(b, 0, 0)
                for j in range(LEAD):
                    reduce_max(b, 0, 1, j)
                    if j == 3:
                        copy_max(b, 0, 0)
                dve.wait_ge(y_stored, 16 * (NCH * b + 1))
                attention_steps(dve, step(b))
                fold_denominator(b, NCH - 1, PAIRS - 1)
                for q in range(PARTS):
                    reciprocal(b, NCH - 1, PAIRS - 1, q)
                count = 2 * NCH * b
                first_norm(b * NCH, 0, count)
                for c in range(NCH):
                    n = b * NCH + c
                    if c >= 1:
                        second_sum(n - 1, c - 1, count + 2 * c)
                    for j in range(JT):
                        split_square(n, j)
                        if j == JT // 2 - 1 and c >= 1:
                            second_norm(n - 1, count + 2 * c)
                    if c + 1 < NCH:
                        first_norm(n + 1, c + 1, count + 2 * c + 1)
                second_sum((b + 1) * NCH - 1, NCH - 1, count + 2 * NCH - 1)
                second_norm((b + 1) * NCH - 1, count + 2 * NCH - 1)


def has_q(c, p):
    return not (isinstance(c, int) and c == NCH - 1 and p >= 1)


def raw_words(ap):
    return ap.bitcast(F32)


def rotary_tables():
    inv = (np.float32(1) / np.power(10000.0, np.arange(0, ROT, 2) / ROT).astype(np.float32)).astype(np.float32)
    angle = (np.arange(SEQ, dtype=np.float32)[None, :] * inv[:, None]).astype(np.float64)
    cos, sin = np.ones((P, SEQ), np.float32), np.zeros((P, SEQ), np.float32)
    h = ROT // 2
    for base in (0, D):
        cos[base:base + h] = cos[base + h:base + 2 * h] = np.cos(angle)
        sin[base:base + h] = -np.sin(angle)
        sin[base + h:base + 2 * h] = np.sin(angle)
    return cos, sin


def kernel(**inputs):
    import concourse.bacc as _bacc
    from concourse.bass_utils import run_bass_kernel_spmd as _run

    a = {k: np.asarray(v) for k, v in inputs.items()}
    x = a["L0_attn_hidden_states"].reshape(BATCH * SEQ, HID)
    cos, sin = rotary_tables()
    arrays = {
        "x": x, "xT": x.T, "wq": a["L0_attn_Wq"], "wk": a["L0_attn_Wk"], "wv": a["L0_attn_Wv"],
        "wo": a["L0_attn_Wo"], "fast_bT": a["L0_ffn_fast_b"].T, "w_fc": a["L0_ffn_w_fc"],
        "w_proj": a["L0_ffn_w_proj"], "uT": a["L0_ffn_u"].T, "v_lr": a["L0_ffn_v"],
        "gate": np.broadcast_to(a["L0_ffn_gate"].reshape(1, 1), (P, 1)),
        "cos_t": cos, "sin_t": sin, "ident_in": np.eye(P, dtype=np.float32),
    }
    arrays = {k: np.ascontiguousarray(v) for k, v in arrays.items()}
    nc = _bacc.Bacc("TRN2", target_bir_lowering=False, num_devices=1)
    aps = {k: nc.dram_tensor(f"in_{k}", v.shape, mybir.dt.from_np(v.dtype), kind="ExternalInput").ap()
           for k, v in arrays.items()}
    out = nc.dram_tensor("out_y", (BATCH * SEQ, HID), F32, kind="ExternalOutput").ap()
    layer_kernel(nc, out=out, **aps)
    r = _run(nc, [{f"in_{k}": v for k, v in arrays.items()}], core_ids=[0])
    return r.results[0]["out_y"].reshape(BATCH, SEQ, HID)
```

```python
from contextlib import ExitStack

import numpy as np

import concourse.bass as bass
from concourse import mybir

F32 = mybir.dt.float32
F32R = mybir.dt.float32r
ALU = mybir.AluOpType
ACT = mybir.ActivationFunctionType
AX_X = mybir.AxisListType.X

P = 128
BATCH, SEQ, HID = 2, 2048, 256
HEADS, KVH, D = 8, 2, 64
ROT = D // 4
FFN, RANK = 1024, 16
EPS = 1e-5
CHUNK = 512
NCH = SEQ // CHUNK
PAIRS = HEADS // 2
UNITS = NCH * PAIRS
STEPS = SEQ // P
HC = HID // P
KEYCH = SEQ // CHUNK
TILES = CHUNK // P
MAXES = 2 * TILES * KEYCH
JT = FFN // P
STAGES = NCH + UNITS
RING = 4
SLOTS = 4
LEAD = 12
HEAD = 12
RECIP_STEPS = (4, 5, 8, 10)
PARTS = len(RECIP_STEPS)
AHEAD = 3
PRIME = 4


def done(n):
    return n + PRIME


def attention_steps(eng, emit):
    for k in range(HEAD):
        emit(0, k)
    with eng.Fori(0, NCH - 1) as c:
        for k in range(HEAD, HEAD + PAIRS * STEPS):
            emit(c, k)
    for k in range(HEAD, PAIRS * STEPS):
        emit(NCH - 1, k)


def first(c, p):
    return isinstance(c, int) and c == 0 and p == 0


def exists(c, p, ahead):
    return not (isinstance(c, int) and c == NCH - 1 and p + ahead >= PAIRS)


def layer_kernel(nc, x, xT, wq, wk, wv, wo, fast_bT, w_fc, w_proj, uT, v_lr, gate, tables, ident_in, out):
    ctx = ExitStack()
    with ctx:
        def sb(name, shape, dt=F32):
            return ctx.enter_context(nc.sbuf_tensor(name, shape, dt))

        def ps(name, shape):
            return ctx.enter_context(nc.psum_tensor(name, shape, F32))

        def sem(name):
            return ctx.enter_context(nc.semaphore(name))

        wqg_sb = sb("wqg_sb", [P, HC, 2 * HEADS * D])
        wk_sb = sb("wk_sb", [P, HC, P])
        wv_sb = sb("wv_sb", [P, HC, P])
        wo_sb = sb("wo_sb", [P, PAIRS, HID])
        wfcT = sb("wfcT", [P, HC, FFN])
        wpT = sb("wpT", [P, JT, HID], F32R)
        wp_scale = sb("wp_scale", [P, HID])
        ident = sb("ident", [P, P])
        ones = sb("ones", [P, D])
        gate_sb = sb("gate_sb", [P, 1])
        xT_sb = sb("xT_sb", [P, HC, SEQ])
        kab = sb("kab", [P, 2, KVH, SEQ], F32R)
        ka = kab[:, 0, :, :]
        kb = kab[:, 1, :, :]
        v_sb = sb("v_sb", [P, STEPS, P])
        qa = sb("qa", [P, PAIRS, 2, CHUNK], F32R)
        qb = sb("qb", [P, PAIRS, 2, CHUNK], F32R)
        og = sb("og", [P, UNITS, CHUNK])
        tables_sb = sb("tables_sb", [P, 2, 2, CHUNK])
        raw_sb = sb("raw_sb", [P, 2, CHUNK])
        rot_sb = sb("rot_sb", [P, 2, CHUNK])
        high_sb = sb("high_sb", [P, 2, CHUNK], F32R)
        low_sb = sb("low_sb", [P, 2, CHUNK], F32R)
        probs = sb("probs", [P, RING, 2 * CHUNK])
        acc = sb("acc", [P, 2, 2 * CHUNK])
        maxp = sb("maxp", [P, 2, MAXES])
        max8 = sb("max8", [P, 2 * TILES])
        mrow = sb("mrow", [2 * TILES, P], F32R)
        oge = sb("oge", [P, 3, CHUNK])
        o_sb, g_sb, e_sb = oge[:, 0, :], oge[:, 1, :], oge[:, 2, :]
        stats = sb("stats", [P, TILES, 6])
        mv = sb("mv", [P, TILES, 2])
        var_eps = sb("var_eps", [P, TILES])
        std = sb("std", [P, TILES])
        rstd = sb("rstd", [P, TILES])
        scales = sb("scales", [P, 3, JT + HC])

        probs_halves = probs[:, :, :].rearrange("p r (h n) -> p r h n", h=2)
        acc_halves = acc[:, :, :].rearrange("p r (h n) -> p r h n", h=2)
        table = [tables_sb[:, i, :, :] for i in range(2)] + [probs_halves[:, i, :, :] for i in range(2)]
        raw = [raw_sb[:, i, :] for i in range(2)] + [probs_halves[:, 2, i, :] for i in range(2)]
        rot = [rot_sb[:, i, :] for i in range(2)] + [probs_halves[:, 3, i, :] for i in range(2)]
        high = [high_sb[:, i, :] for i in range(2)] + [acc_halves[:, i, 0, :].bitcast(F32R) for i in range(2)]
        low = [low_sb[:, i, :] for i in range(2)] + [acc_halves[:, i, 1, :].bitcast(F32R) for i in range(2)]

        attnT = probs[:, 0, :].rearrange("p (h n) -> p h n", h=HC)
        y1 = probs[:, 1, :].rearrange("p (i c) -> p i c", c=HID)
        x1s = [probs[:, 2 + i, :].rearrange("p (i c) -> p i c", c=HID) for i in range(2)]
        x1_high = low_sb[:, :, :]
        x1_low = high_sb[:, :, :]
        w_high, w_low = [ka[:, i, :].rearrange("p (h n) -> p h n", h=HC) for i in range(2)]
        y2 = oge[:, 0:2, :].rearrange("p a (b c) -> p (a b) c", c=HID)
        xres = acc[:, 0, :].rearrange("p (i c) -> p i c", c=HID)
        yout = acc[:, 1, :].rearrange("p (i c) -> p i c", c=HID)
        relu_ring = [raw[0], raw[1]] + [v_sb[:, i * TILES:(i + 1) * TILES, :].rearrange("p i n -> p (i n)")
                                        for i in range(2)]
        sq_high = qa[:, :, :, :].rearrange("p a h n -> p (a h) n")
        sq_low = qb[:, :, :, :].rearrange("p a h n -> p (a h) n")
        wfc_nat = og[:, 0:4, :].rearrange("p a (b c) -> p (a b) c", c=HID)
        wfc_w = og[:, 4:8, :].rearrange("p a (b c) -> p (a b) c", c=HID)
        wp_nat = og[:, 8:12, :].rearrange("p (a b) c -> p a (b c)", a=HC)
        wp_w = og[:, 12:16, :].rearrange("p (a b) c -> p a (b c)", a=HC)
        spare = oge[:, :, :].rearrange("p a n -> p (a n)")
        uT_sb = spare[0:RANK, 0:FFN]
        v_lr_sb = spare[0:RANK, FFN:FFN + HID]
        bv_sb = spare[0:RANK, FFN + HID:FFN + 2 * HID]
        fbT_sb = maxp[0:RANK, 0, 0:RANK]

        sc = ps("sc", [P, 4, CHUNK])
        mx = ps("mx", [P, 2, CHUNK])
        ob = ps("ob", [P, CHUNK])
        misc = ps("misc", [P, CHUNK])

        wfc_loaded = sem("wfc_loaded")
        ffn_loaded = sem("ffn_loaded")
        weights_loaded = sem("weights_loaded")
        setup_pe = sem("setup_pe")
        setup_act = sem("setup_act")
        setup_dve = sem("setup_dve")
        ones_set = sem("ones_set")
        rot_cleared = sem("rot_cleared")
        xT_loaded = sem("xT_loaded")
        tables_loaded = [sem(f"tables_loaded{i}") for i in range(SLOTS)]
        rot_placed = [sem(f"rot_placed{i}") for i in range(SLOTS)]
        placed = [sem(f"placed{i}") for i in range(SLOTS)]
        m_placed = sem("m_placed")
        xres_loaded = sem("xres_loaded")
        y_stored = sem("y_stored")

        q_ready = sem("q_ready")
        v_ready = sem("v_ready")
        max_ready = sem("max_ready")
        mt_ready = sem("mt_ready")
        scores_ready = sem("scores_ready")
        pv_done = sem("pv_done")
        den_ready = sem("den_ready")
        gate_ready = sem("gate_ready")
        attn_ready = sem("attn_ready")
        tr_ready = sem("tr_ready")
        x1t_ready = sem("x1t_ready")
        ffn1_ready = sem("ffn1_ready")
        ffn2_ready = sem("ffn2_ready")
        w_rounded = sem("w_rounded")
        w_split = sem("w_split")
        x1t_split = sem("x1t_split")
        PE_SEMS = [q_ready, v_ready, max_ready, mt_ready, scores_ready, pv_done, den_ready, gate_ready,
                   attn_ready, tr_ready, x1t_ready, ffn1_ready, ffn2_ready]

        q_copied = sem("q_copied")
        v_copied = sem("v_copied")
        rounded = [sem(f"rounded{i}") for i in range(SLOTS)]
        probs_ready = sem("probs_ready")
        gate_copied = sem("gate_copied")
        o_copied = sem("o_copied")
        attn_copied = sem("attn_copied")
        x1t_copied = sem("x1t_copied")
        relu_done = sem("relu_done")
        std_done = sem("std_done")
        sq_rounded = sem("sq_rounded")
        ACT_SEMS = [q_copied, v_copied, *rounded, probs_ready, gate_copied, o_copied, attn_copied,
                    x1t_copied, relu_done, sq_rounded, std_done, w_rounded]

        maxed = sem("maxed")
        max8_done = sem("max8_done")
        m_copied = sem("m_copied")
        sum_b = sem("sum_b")
        den_used = sem("den_used")
        recip_done = sem("recip_done")
        ln_chain = sem("ln_chain")
        res_done = sem("res_done")
        y2_done = sem("y2_done")
        y2_summed = sem("y2_summed")
        sq_split = sem("sq_split")
        var_ready = sem("var_ready")
        x1_done = sem("x1_done")
        post_done = sem("post_done")
        DVE_SEMS = [maxed, max8_done, m_copied, sum_b, den_used, recip_done, ln_chain, res_done, sq_split, y2_summed,
                    y2_done, var_ready, x1_done, post_done, x1t_split]

        sum_a = sem("sum_a")
        og_step = sem("og_step")
        squared = sem("squared")
        rope_step = [sem(f"rope_step{i}") for i in range(SLOTS)]
        low_done = [sem(f"low_done{i}") for i in range(SLOTS)]
        POOL_SEMS = [w_split, sum_a, og_step, squared, *rope_step, *low_done]

        x_tiles = x.rearrange("(n i p) c -> p n i c", p=P, i=TILES)
        out_tiles = out.rearrange("(n i p) c -> p n i c", p=P, i=TILES)
        xT_v = xT.rearrange("(h p) t -> p h t", p=P)

        FRONT = [("q", 0, 0, "dve"), ("k", 0, 1, "dve"), ("k", 1, 2, "pool"), ("k", 2, 3, "pool"),
                 ("k", 3, 0, "pool"), ("q", 1, 1, "pool"), ("q", 2, 0, "pool")]
        PRO = len(FRONT)
        per_batch = [sum(f[2] == slot for f in FRONT) + (UNITS - AHEAD + slot) // 2 * (slot < 2) for slot in range(SLOTS)]

        def front(s):
            return FRONT[s][2], sum(f[2] == FRONT[s][2] for f in FRONT[:s])

        def behind(p, c):
            slot = (p + 1) % 2
            return slot, sum(f[2] == slot for f in FRONT) + c * (PAIRS // 2) + p // 2

        def uses(stage, b):
            return b * per_batch[stage[0]] + stage[1]

        def placed_before(stage, b, more=0):
            slot, local = stage
            local = local + more
            k_at = [f[0] for f in FRONT if f[2] == slot].index("k")
            k_counted = not isinstance(local, int) or local > k_at
            return 96 + 96 * local - 32 * k_counted + b * (96 * per_batch[slot] - 32)

        def rope(eng, stage, b):
            slot, i = stage[0], uses(stage, b)
            eng.wait_ge(rot_placed[slot], 32 * (i + 1))
            eng.wait_ge(tables_loaded[slot], 16 * (i + 1))
            eng.tensor_tensor(raw[slot], raw[slot], table[slot][:, 0, :], ALU.mult).then_inc(rope_step[slot], 1)
            eng.tensor_tensor(rot[slot], rot[slot], table[slot][:, 1, :], ALU.mult).then_inc(rope_step[slot], 1)

        def rope_add(eng, stage, b):
            slot, i = stage[0], uses(stage, b)
            eng.wait_ge(rope_step[slot], done(3 * i + 2))
            eng.tensor_tensor(raw[slot], raw[slot], rot[slot], ALU.add).then_inc(rope_step[slot], 1)

        def rope_low(eng, stage, b):
            slot, i = stage[0], uses(stage, b)
            eng.wait_ge(rounded[slot], done(i + 1))
            eng.wait_ge(placed[slot], placed_before(stage, b))
            eng.tensor_tensor(low[slot], raw[slot], high[slot].bitcast(F32), ALU.subtract).then_inc(low_done[slot], 1)

        def add_exponentials(eng, ops, b, c, k, hd, summed):
            p, t = k // STEPS, k % STEPS
            n = (b * UNITS + c * PAIRS) * STEPS + k
            cols = slice(hd * CHUNK, (hd + 1) * CHUNK)
            total, part = acc[:, p % 2, cols], probs[:, k % RING, cols]
            if t == 1:
                eng.wait_ge(probs_ready, done(n + 1))
                eng.wait_ge(den_ready, done(b * UNITS + c * PAIRS + p - 1))
                ops.tensor_tensor(total, probs[:, (k - 1) % RING, cols], part, ALU.add).then_inc(summed, 2)
            elif t > 1:
                eng.wait_ge(probs_ready, done(n + 1))
                eng.wait_ge(summed, done(n))
                ops.tensor_tensor(total, total, part, ALU.add).then_inc(summed, 1)

        FRONT_BANKS = [misc, ob]
        MAX_PAIRS = [mx[:, :, :], sc[:, 2:4, :]]

        ROTARY_ROWS = slice(0, P, 4)

        block = ctx.enter_context(nc.Block())

        @block.sync
        def _(sp):
            sp.sem_inc(m_placed, 16)
            sp.sem_inc(y_stored, 16)
            for slot in range(SLOTS):
                sp.sem_inc(placed[slot], 96)
            sp.dma_start(wfc_nat, w_fc.rearrange("(j p) c -> p j c", p=P)).then_inc(wfc_loaded, 16)
            for dst, src in (
                    (fbT_sb, fast_bT), (v_lr_sb, v_lr), (gate_sb[:, :], gate), (uT_sb, uT), (ident[:, :], ident_in),
                    (wp_nat, w_proj.rearrange("(h p) j -> p h j", p=P))):
                sp.dma_start(dst, src).then_inc(ffn_loaded, 16)
            sp.dma_start(xT_sb[:, :, :], xT_v[:, :, 0:SEQ]).then_inc(xT_loaded, 16)
            for dst, src in (
                    (wqg_sb[:, :, :], wq.rearrange("(h p) n -> p h n", p=P)),
                    (wk_sb[:, :, :], wk.rearrange("(h p) n -> p h n", p=P)),
                    (wv_sb[:, :, :], wv.rearrange("(h p) n -> p h n", p=P)),
                    (wo_sb[:, :, :], wo.rearrange("(h p) n -> p h n", p=P))):
                sp.dma_start(dst, src).then_inc(weights_loaded, 16)

            def load_tables(stage, b, chunk, rows=slice(None)):
                slot = stage[0]
                sp.wait_ge(low_done[slot], done(uses(stage, b)))
                sp.dma_start(table[slot][rows], tables[rows, bass.ds(chunk, 1), :, :].rearrange("p a b n -> p (a b) n"))\
                  .then_inc(tables_loaded[slot], 16)

            def swap_rows(stage, number, b):
                slot = stage[0]
                sp.wait_ge(q_copied, done(b * STAGES + number + 1))
                for to, frm in ((0, 4), (4, 0)):
                    sp.dma_start(rot[slot][to::8], raw[slot][frm::8]).then_inc(rot_placed[slot], 16)

            def place(stage, b, targets):
                slot = stage[0]
                sp.wait_ge(low_done[slot], done(uses(stage, b) + 1))
                for part, hd, dst in targets:
                    src = raw_words(part[slot][hd * D:(hd + 1) * D])
                    if len(dst.shape) == 3:
                        src = src.unsqueeze(1).broadcast_to([D, 2, CHUNK])
                    sp.dma_start(raw_words(dst), src).then_inc(placed[slot], 16)

            def k_targets(n):
                keys = slice(n * CHUNK, (n + 1) * CHUNK)
                return [t for g in range(KVH) for t in ((high, g, kab[0:D, :, g, keys]), (low, g, ka[D:P, g, keys]))]

            def q_targets(slot):
                return [t for hd in range(2) for t in (
                    (high, hd, qa[0:D, slot, hd, :]), (high, hd, qa[D:P, slot, hd, :]), (low, hd, qb[0:D, slot, hd, :]))]

            def place_max(b, c, p):
                sp.wait_ge(m_copied, done(b * UNITS + c * PAIRS + p + 1))
                sp.dma_start(raw_words(qb[D:D + 1, p % PAIRS, :, :]), raw_words(mrow[:, :])).then_inc(m_placed, 16)

            def step(b):
                def emit(c, k):
                    p, t = k // STEPS, k % STEPS
                    unit = b * UNITS + c * PAIRS + p
                    if t == 2 and has_q(c, p):
                        load_tables(behind(p, c), b, c + (p + AHEAD) // PAIRS, ROTARY_ROWS)
                    if t == 6 and has_q(c, p):
                        swap_rows(behind(p, c), PRO + c * PAIRS + p, b)
                    if t == 14 and has_q(c, p):
                        place(behind(p, c), b, q_targets((p + AHEAD) % PAIRS))
                    if t == 13 and exists(c, p, 1):
                        place_max(b, c, p + 1)
                return emit

            for slot in range(2):
                load_tables((slot, 0), 0, 0)

            with sp.Fori(0, BATCH) as b:
                sp.wait_ge(ones_set, 3)
                sp.wait_ge(y2_summed, done(b * NCH))

                def front_tables(s):
                    load_tables(front(s), b, FRONT[s][1] if FRONT[s][0] == "k" else 0,
                                ROTARY_ROWS if FRONT[s][2] < 2 else slice(None))

                def front_swap(s):
                    swap_rows(front(s), s, b)

                def front_place(s):
                    what, n = FRONT[s][0:2]
                    place(front(s), b, k_targets(n) if what == "k" else q_targets(n))

                front_swap(0)
                front_swap(1)
                front_tables(2)
                front_swap(2)
                front_tables(3)
                front_swap(3)
                front_place(0)
                front_place(1)
                front_tables(4)
                front_swap(4)
                front_tables(5)
                front_place(2)
                front_swap(5)
                front_place(3)
                front_place(4)
                front_tables(6)
                front_swap(6)
                front_place(5)
                front_place(6)
                place_max(b, 0, 0)
                attention_steps(sp, step(b))

                def load_residual(c):
                    n = b * NCH + c
                    if c == 0:
                        sp.wait_ge(og_step, done(2 * UNITS * (b + 1)))
                    sp.wait_ge(res_done, done(n * TILES))
                    sp.dma_start(xres, x_tiles[:, n, :, :]).then_inc(xres_loaded, 16)

                load_residual(0)
                with sp.If(b < BATCH - 1):
                    sp.wait_ge(gate_ready, done((b + 1) * UNITS))
                    sp.dma_start(xT_sb[:, :, :], xT_v[:, :, SEQ:2 * SEQ]).then_inc(xT_loaded, 16)
                    for slot in range(2):
                        sp.dma_start(table[slot][ROTARY_ROWS], tables[ROTARY_ROWS, 0, :, :])\
                          .then_inc(tables_loaded[slot], 16)
                load_residual(1)
                for c in range(NCH):
                    n = b * NCH + c
                    sp.wait_ge(post_done, done(n + 1))
                    sp.dma_start(out_tiles[:, n, :, :], yout).then_inc(y_stored, 16)
                    if c + 2 < NCH:
                        load_residual(c + 2)
            sp.wait_ge(y_stored, 16 * (BATCH * NCH + 1))

        @block.tensor
        def _(pe):
            for s in PE_SEMS:
                pe.sem_inc(s, PRIME)

            pe.wait_ge(ffn_loaded, 16 * 6)
            nc.tensor.matmul(misc[0:RANK, 0:HID], fbT_sb, v_lr_sb, start=True, stop=True).then_inc(setup_pe, 1)
            pe.wait_ge(setup_act, 1)
            for j in range(JT):
                mm = nc.tensor.matmul(sc[:, j // 2, (j % 2) * HID:(j % 2 + 1) * HID],
                                      uT_sb[:, j * P:(j + 1) * P], bv_sb, start=True, stop=True)
            mm.then_inc(setup_pe, 1)
            pe.wait_ge(setup_dve, 1)
            banks = [mx[:, 0, :], mx[:, 1, :], ob[:, :], misc[:, :]]
            for h in range(HC):
                for j in range(JT):
                    tr = nc.tensor.transpose(banks[2 * h + j // 4][:, (j % 4) * P:(j % 4 + 1) * P],
                                             wfc_w[:, j, h * P:(h + 1) * P], ident[:, :])
            tr.then_inc(setup_pe, 1)
            pe.wait_ge(setup_dve, 2)
            for j in range(JT):
                for h in range(HC):
                    tr = nc.tensor.transpose(sc[:, j // 2, (j % 2) * HID + h * P:(j % 2) * HID + (h + 1) * P],
                                             wp_w[:, h, j * P:(j + 1) * P], ident[:, :])
            pe.wait_ge(setup_act, 2)
            pe.wait_ge(ones_set, 3)
            for i in range(2):
                mm = nc.tensor.matmul(misc[i * D:(i + 1) * D, 0:HID], ones[:, :], wp_scale[:, :],
                                      start=True, stop=True)
            mm.then_inc(setup_pe, 1)
            pe.wait_ge(setup_act, 3)

            def project(w, col, chunk, semaphore, bank=misc):
                for h in range(HC):
                    mm = nc.tensor.matmul(bank[:, :], w[:, h, col:col + P],
                                          xT_sb[:, h, bass.ds(chunk * CHUNK, CHUNK)],
                                          start=(h == 0), stop=(h == HC - 1))
                mm.then_inc(semaphore, 1)

            def v_group(g, b):
                if g >= 2:
                    pe.wait_ge(v_copied, done(b * TILES + g - 1))
                for i in range(TILES):
                    tile = g * TILES + i
                    for h in range(HC):
                        mm = nc.tensor.matmul(sc[:, g % 2, i * P:(i + 1) * P], xT_sb[:, h, tile * P:(tile + 1) * P],
                                              wv_sb[:, h, :], start=(h == 0), stop=(h == HC - 1))
                mm.then_inc(v_ready, 1)

            def row_max(b, c, p, j):
                kc, hd, st = j // (2 * TILES), j // TILES % 2, j % TILES
                unit = b * UNITS + c * PAIRS + p
                if j == 0 and not first(c, p):
                    stage = behind(p - AHEAD, c)
                    pe.wait_ge(placed[stage[0]], placed_before(stage, b, 1))
                pe.wait_ge(maxed, done(unit * MAXES + j - 1))
                nc.tensor.matmul(mx[:, j % 2, :], qa[:, p % PAIRS, hd, st * P:(st + 1) * P],
                                 ka[:, p % PAIRS // 2, kc * CHUNK:(kc + 1) * CHUNK],
                                 start=True, stop=True).then_inc(max_ready, 1)

            def max_transpose(b, c, p):
                pe.wait_ge(max8_done, done(b * UNITS + c * PAIRS + p + 1))
                nc.tensor.transpose(misc[0:2 * TILES, 0:P], max8[:, :], ident[:, :]).then_inc(mt_ready, 1)

            def scores(b, c, k):
                p, t = k // STEPS, k % STEPS
                n = (b * UNITS + c * PAIRS) * STEPS + k
                keys, kv = slice(t * P, (t + 1) * P), p % PAIRS // 2
                if t == 0:
                    pe.wait_ge(m_placed, 16 * (b * UNITS + c * PAIRS + p + 2))
                pe.wait_ge(probs_ready, done(n - 1))
                for hd in range(2):
                    nc.tensor.matmul(sc[:, 2 * (k % 2) + hd, :], ka[:, kv, keys], qa[:, p % PAIRS, hd, :],
                                     start=True, stop=False)
                for hd in range(2):
                    mm = nc.tensor.matmul(sc[:, 2 * (k % 2) + hd, :], kb[0:D + 1, kv, keys],
                                          qb[0:D + 1, p % PAIRS, hd, :], start=False, stop=True)
                mm.then_inc(scores_ready, 1)

            def weighted_v(b, c, k):
                p, t = k // STEPS, k % STEPS
                n = (b * UNITS + c * PAIRS) * STEPS + k
                kv = p % PAIRS // 2
                pe.wait_ge(probs_ready, done(n + 1))
                if t == 0:
                    pe.wait_ge(o_copied, done(b * UNITS + c * PAIRS + p))
                for hd in range(2):
                    mm = nc.tensor.matmul(ob[hd * D:(hd + 1) * D, :], v_sb[:, t, kv * D:(kv + 1) * D],
                                          probs[:, k % RING, hd * CHUNK:(hd + 1) * CHUNK],
                                          start=(t == 0), stop=(t == STEPS - 1))
                mm.then_inc(pv_done, 1)

            def denominators(b, c, p):
                unit = b * UNITS + c * PAIRS + p
                pe.wait_ge(sum_a, done((unit + 1) * STEPS))
                pe.wait_ge(sum_b, done((unit + 1) * STEPS))
                for hd in range(2):
                    mm = nc.tensor.matmul(misc[hd * D:(hd + 1) * D, :], ones[:, :],
                                          acc[:, p % 2, hd * CHUNK:(hd + 1) * CHUNK], start=True, stop=True)
                mm.then_inc(den_ready, 1)

            def step(b):
                def emit(c, k):
                    p, t = k // STEPS, k % STEPS
                    unit = b * UNITS + c * PAIRS + p

                    def look_ahead(j):
                        ahead = 1 + j // MAXES
                        if exists(c, p, ahead):
                            row_max(b, c, p + ahead, j % MAXES)

                    if not (isinstance(c, int) and c == NCH - 1 and k == PAIRS * STEPS - 1):
                        scores(b, c, k + 1)
                    look_ahead(LEAD + 2 * t)
                    if t % 2 == 0:
                        look_ahead(LEAD + 2 * t + 1)
                    if t % 2:
                        weighted_v(b, c, k - 1)
                        weighted_v(b, c, k)
                    if t == 1 and not first(c, p):
                        pe.wait_ge(gate_copied, done(unit))
                        denominators(b, c, p - 1)
                    if t == 5 and has_q(c, p):
                        if first(c, p):
                            pe.wait_ge(m_copied, done(unit + 1))
                        else:
                            pe.wait_ge(den_used, done(unit))
                        project(wqg_sb, (p + AHEAD) % PAIRS * P, c + (p + AHEAD) // PAIRS, q_ready)
                    if t == 11 and exists(c, p, 1):
                        if has_q(c, p):
                            pe.wait_ge(q_copied, done(b * STAGES + c * PAIRS + PRO + p + 1))
                        else:
                            pe.wait_ge(den_used, done(unit))
                        max_transpose(b, c, p + 1)
                    if t == 13:
                        if exists(c, p, 1):
                            pe.wait_ge(m_copied, done(unit + 2))
                        else:
                            pe.wait_ge(den_used, done(unit))
                        project(wqg_sb, HEADS * D + p % PAIRS * P, c, gate_ready)
                    if t % 2:
                        look_ahead(LEAD + 2 * t + 1)
                return emit

            def output_projection(n, c):
                pe.wait_ge(attn_copied, done(n * HC))
                if c >= 2:
                    pe.wait_ge(x1t_split, done((n - 1) * HC))
                for h in range(HC):
                    for p in range(PAIRS):
                        mm = nc.tensor.matmul(sc[:, h, :], wo_sb[:, p, h * P:(h + 1) * P],
                                              og[:, c * PAIRS + p, :], start=(p == 0), stop=(p == PAIRS - 1))
                    mm.then_inc(attn_ready, 1)

            def output_transposes(n):
                pe.wait_ge(attn_copied, done((n + 1) * HC))
                pe.wait_ge(res_done, done(n * TILES))
                for i in range(TILES):
                    for h in range(HC):
                        tr = nc.tensor.transpose(sc[:, 2 + i // 2, (i % 2) * HID + h * P:(i % 2) * HID + (h + 1) * P],
                                                 attnT[:, h, i * P:(i + 1) * P], ident[:, :])
                    if i % 2:
                        tr.then_inc(tr_ready, 1)

            def x1_transposes(n, x1, attention_copies):
                pe.wait_ge(x1_done, done((n + 1) * TILES))
                pe.wait_ge(attn_copied, done(attention_copies))
                for h in range(HC):
                    for i in range(TILES):
                        tr = nc.tensor.transpose(sc[:, h, i * P:(i + 1) * P], x1[:, i, h * P:(h + 1) * P], ident[:, :])
                    tr.then_inc(x1t_ready, 1)

            def ffn_up(n):
                for j in range(JT):
                    if j >= 2:
                        pe.wait_ge(relu_done, done(n * JT + j - 1))
                    else:
                        pe.wait_ge(relu_done, done(n * JT))
                    for w, x1t in ((w_high, x1_high), (w_low, x1_high), (w_high, x1_low)):
                        for h in range(HC):
                            if j == 0 and w is w_high:
                                pe.wait_ge(x1t_copied if x1t is x1_high else x1t_split, done(n * HC + h + 1))
                            mm = nc.tensor.matmul(mx[:, j % 2, :], w[:, h, j * P:(j + 1) * P], x1t[:, h, :],
                                                  start=(w is w_high and x1t is x1_high and h == 0),
                                                  stop=(x1t is x1_low and h == HC - 1))
                    mm.then_inc(ffn1_ready, 1)

            def ffn_down(n, hidden_tiles):
                for j in hidden_tiles:
                    if j == 0:
                        pe.wait_ge(y2_done, done(n * TILES))
                    pe.wait_ge(sq_split, done(n * JT + j + 1))
                    for i in range(TILES):
                        bank = (ob if i < 2 else misc)[:, (i % 2) * HID:(i % 2 + 1) * HID]
                        for part in (sq_high, sq_low):
                            mm = nc.tensor.matmul(bank, part[:, j, i * P:(i + 1) * P], wpT[:, j, :],
                                                  start=(j == 0 and part is sq_high and i % 2 == 0),
                                                  stop=(j == JT - 1 and part is sq_low and i % 2 == 1))
                        if j == JT - 1 and i % 2:
                            mm.then_inc(ffn2_ready, 1)

            with pe.Fori(0, BATCH) as b:
                pe.wait_ge(xT_loaded, 16 * (b + 1))
                pe.wait_ge(y2_done, done(b * NCH * TILES))
                pe.wait_ge(weights_loaded, 16 * 4)

                def front_project(s):
                    what, n = FRONT[s][0:2]
                    if s >= 2:
                        pe.wait_ge(q_copied, done(b * STAGES + s - 1))
                    if what == "k":
                        project(wk_sb, 0, n, q_ready, FRONT_BANKS[s % 2])
                    else:
                        project(wqg_sb, n * P, 0, q_ready, FRONT_BANKS[s % 2])

                def front_pair(p, i):
                    pe.wait_ge(maxed, done((b * UNITS + p) * MAXES + (2 * (i - 1) if p or i else 0)))
                    for half in range(2):
                        hd, st, n = i % TILES // 2, i % 2 * 2 + half, i // TILES
                        mm = nc.tensor.matmul(MAX_PAIRS[i % 2][:, half, :], qa[:, p, hd, st * P:(st + 1) * P],
                                              ka[:, p // 2, n * CHUNK:(n + 1) * CHUNK], start=True, stop=True)
                    mm.then_inc(max_ready, 2)

                def front_maxima(n):
                    s = [f[0:2] for f in FRONT].index(("k", n))
                    if n == 0:
                        pe.wait_ge(placed[0], placed_before(front(0), b, 1))
                    pe.wait_ge(placed[FRONT[s][2]], placed_before(front(s), b, 1))
                    for i in range(TILES * n, TILES * (n + 1)):
                        front_pair(0, i)

                for s in range(PRO - 1):
                    front_project(s)
                v_group(0, b)
                v_group(1, b)
                front_maxima(0)
                v_group(2, b)
                front_maxima(1)
                v_group(3, b)
                front_project(PRO - 1)
                front_maxima(2)
                front_maxima(3)
                stage = front(5)
                pe.wait_ge(placed[stage[0]], placed_before(stage, b, 1))
                for i in range(2):
                    front_pair(1, i)
                pe.wait_ge(q_copied, done(b * STAGES + PRO))
                max_transpose(b, 0, 0)
                for i in range(2, LEAD // 2):
                    front_pair(1, i)
                pe.wait_ge(v_copied, done((b + 1) * TILES))
                scores(b, 0, 0)
                pe.wait_ge(maxed, done((b * UNITS + 1) * MAXES + LEAD))
                attention_steps(pe, step(b))
                pe.wait_ge(gate_copied, done((b + 1) * UNITS))
                denominators(b, NCH - 1, PAIRS - 1)
                first_n = b * NCH
                output_projection(first_n, 0)
                output_transposes(first_n)
                output_projection(first_n + 1, 1)
                x1_transposes(first_n, x1s[0], (first_n + 2) * HC)
                pe.wait_ge(w_split, done(4 * (b + 1)))
                for c in range(NCH):
                    ffn_up(first_n + c)
                    if c + 1 < NCH:
                        output_transposes(first_n + c + 1)
                    if c + 2 < NCH:
                        if c + 2 == NCH - 1:
                            pe.wait_ge(og_step, done(2 * UNITS * (b + 1)))
                        output_projection(first_n + c + 2, c + 2)
                    ffn_down(first_n + c, range(JT - 2))
                    if c + 1 < NCH:
                        x1_transposes(first_n + c + 1, x1s[(c + 1) % 2], (first_n + min(c + 3, NCH)) * HC)
                    ffn_down(first_n + c, range(JT - 2, JT))

        @block.scalar
        def _(act):
            for s in ACT_SEMS:
                act.sem_inc(s, PRIME)
            act.wait_ge(setup_pe, 1)
            nc.scalar.activation(bv_sb, misc[0:RANK, 0:HID], ACT.Copy, scale=gate_sb[0:RANK, 0:1]).then_inc(setup_act, 1)
            act.wait_ge(setup_pe, 3)
            for h in range(HC):
                for q, bank in enumerate(([mx[:, 0, :], mx[:, 1, :]], [ob[:, :], misc[:, :]])[h]):
                    last = nc.scalar.copy(wfcT[:, h, q * CHUNK:(q + 1) * CHUNK], bank)
            last.then_inc(setup_act, 1)
            act.wait_ge(setup_pe, 4)
            for q in range(4):
                nc.scalar.copy(wpT[:, 2 * q:2 * q + 2, :], sc[:, q, :].rearrange("p (a c) -> p a c", a=2))
            last = nc.scalar.copy(wp_scale[:, :], misc[:, 0:HID])
            last.then_inc(setup_act, 1)

            def copy_stage(stage, number, b, in_front=False):
                slot = stage[0]
                if slot >= 2:
                    act.wait_ge(rot_cleared, b + 1)
                act.wait_ge(q_ready, done(b * STAGES + number + 1))
                act.wait_ge(low_done[slot], done(uses(stage, b)))
                bank = FRONT_BANKS[number % 2] if in_front else misc
                nc.scalar.copy(raw[slot], bank[:, :]).then_inc(q_copied, 1)

            def round_stage(stage, b):
                slot = stage[0]
                if slot >= 2:
                    act.wait_ge(y_stored, 16 * (NCH * b + 1))
                act.wait_ge(rope_step[slot], done(3 * uses(stage, b) + 3))
                act.wait_ge(placed[slot], placed_before(stage, b))
                nc.scalar.copy(high[slot], raw[slot]).then_inc(rounded[slot], 1)

            def copy_v(g, b):
                act.wait_ge(v_ready, done(b * TILES + g + 1))
                nc.scalar.copy(v_sb[:, g * TILES:(g + 1) * TILES, :],
                               sc[:, g % 2, :].rearrange("p (a c) -> p a c", a=TILES)).then_inc(v_copied, 1)

            def copy_o(b, c, p):
                unit = b * UNITS + c * PAIRS + p
                act.wait_ge(pv_done, done((unit + 1) * STEPS))
                act.wait_ge(og_step, done(2 * unit))
                nc.scalar.copy(o_sb, ob[:, :]).then_inc(o_copied, 1)

            def step(b):
                def emit(c, k):
                    p, t = k // STEPS, k % STEPS
                    unit = b * UNITS + c * PAIRS + p
                    n = (b * UNITS + c * PAIRS) * STEPS + k
                    act.wait_ge(scores_ready, done(n + 1))
                    act.wait_ge(pv_done, done(n + 1 - RING))
                    act.wait_ge(sum_a, done(n + 1 - RING))
                    act.wait_ge(sum_b, done(n + 1 - RING))
                    nc.scalar.activation(probs[:, k % RING, :].rearrange("p (h n) -> p h n", h=2),
                                         sc[:, 2 * (k % 2):2 * (k % 2) + 2, :], ACT.Exp,
                                         scale=float(D) ** -0.5).then_inc(probs_ready, 1)
                    if t == 0 and not first(c, p):
                        copy_o(b, c, p - 1)
                    if t == 6 and has_q(c, p):
                        copy_stage(behind(p, c), PRO + c * PAIRS + p, b)
                    if t == 14:
                        act.wait_ge(gate_ready, done(unit + 1))
                        act.wait_ge(og_step, done(2 * unit))
                        nc.scalar.activation(e_sb, misc[:, :], ACT.Exp, scale=-1.0)
                        nc.scalar.copy(g_sb, misc[:, :]).then_inc(gate_copied, 1)
                    if t == 11 and has_q(c, p):
                        round_stage(behind(p, c), b)
                return emit

            def copy_attention(n):
                act.wait_ge(tr_ready, done(2 * n))
                for h in range(HC):
                    act.wait_ge(attn_ready, done(n * HC + h + 1))
                    nc.scalar.copy(attnT[:, h, :], sc[:, h, :]).then_inc(attn_copied, 1)

            def deviation(count):
                act.wait_ge(var_ready, done(count + 1))
                nc.scalar.activation(std[:, :], var_eps[:, :], ACT.Sqrt).then_inc(std_done, 1)

            def copy_x1(n):
                act.wait_ge(ffn1_ready, done(n * JT))
                for h in range(HC):
                    act.wait_ge(x1t_ready, done(n * HC + h + 1))
                    nc.scalar.copy(x1_high[:, h, :], sc[:, h, :]).then_inc(x1t_copied, 1)

            def relu(n, j):
                act.wait_ge(sq_split, done(n * JT + j + 1 - len(relu_ring)))
                act.wait_ge(ffn1_ready, done(n * JT + j + 1))
                nc.scalar.activation(relu_ring[j % 4], mx[:, j % 2, :], ACT.Relu).then_inc(relu_done, 1)

            def round_square(n, j):
                if j == 0:
                    act.wait_ge(ffn2_ready, done(2 * n))
                act.wait_ge(squared, done(n * JT + j + 1))
                nc.scalar.copy(sq_high[:, j, :], relu_ring[j % 4]).then_inc(sq_rounded, 1)

            with act.Fori(0, BATCH) as b:
                act.wait_ge(y2_summed, done(b * NCH))

                def front_copy(s):
                    copy_stage(front(s), s, b, True)

                def front_round(s):
                    round_stage(front(s), b)

                for s in range(SLOTS):
                    front_copy(s)
                front_round(0)
                front_copy(4)
                front_round(1)
                copy_v(0, b)
                copy_v(1, b)
                front_copy(5)
                front_round(2)
                front_round(3)
                front_round(4)
                copy_v(2, b)
                front_copy(6)
                copy_v(3, b)
                front_round(5)
                front_round(6)
                attention_steps(act, step(b))
                copy_o(b, NCH - 1, PAIRS - 1)
                for q in range(4):
                    h, cols = q // 2, slice(q % 2 * CHUNK, (q % 2 + 1) * CHUNK)
                    nc.scalar.copy(w_high[:, h, cols], wfcT[:, h, cols]).then_inc(w_rounded, 1)
                copy_attention(b * NCH)
                deviation(2 * b * NCH)
                copy_attention(b * NCH + 1)
                for c in range(NCH):
                    n = b * NCH + c
                    copy_x1(n)
                    for j in range(JT + 1):
                        if j < JT:
                            relu(n, j)
                        if j >= 1:
                            round_square(n, j - 1)
                        if j == JT // 2 and c >= 1:
                            deviation(2 * n)
                    if c + 1 < NCH:
                        deviation(2 * n + 1)
                    if c + 2 < NCH:
                        copy_attention(n + 2)
                deviation(2 * (b + 1) * NCH - 1)

        @block.gpsimd
        def _(pool):
            for s in POOL_SEMS:
                pool.sem_inc(s, PRIME)

            def gated(b, c, p):
                unit = b * UNITS + c * PAIRS + p
                pool.wait_ge(recip_done, done(PARTS * (unit + 1)))
                nc.gpsimd.tensor_tensor(e_sb, e_sb, g_sb, ALU.mult).then_inc(og_step, 1)
                pool.wait_ge(og_step, done(2 * unit + 1))
                pool.wait_ge(o_copied, done(unit + 1))
                nc.gpsimd.tensor_tensor(og[:, c * PAIRS + p, :], o_sb, e_sb, ALU.mult)\
                  .then_inc(og_step, 1)

            def step(b):
                def emit(c, k):
                    p, t = k // STEPS, k % STEPS
                    add_exponentials(pool, nc.gpsimd, b, c, k, 0, sum_a)
                    if t == 11 and not first(c, p):
                        gated(b, c, p - 1)
                    if t == 7 and has_q(c, p):
                        rope(nc.gpsimd, behind(p, c), b)
                    if t == 8 and has_q(c, p):
                        rope_add(nc.gpsimd, behind(p, c), b)
                    if t == 12 and has_q(c, p):
                        rope_low(nc.gpsimd, behind(p, c), b)
                return emit

            with pool.Fori(0, BATCH) as b:
                pool.wait_ge(y_stored, 16 * (NCH * b + 1))
                for s in range(PRO):
                    if FRONT[s][3] == "pool":
                        rope(nc.gpsimd, front(s), b)
                        rope_add(nc.gpsimd, front(s), b)
                        rope_low(nc.gpsimd, front(s), b)
                attention_steps(pool, step(b))
                for q in range(4):
                    h, cols = q // 2, slice(q % 2 * CHUNK, (q % 2 + 1) * CHUNK)
                    pool.wait_ge(w_rounded, done(4 * b + q + 1))
                    nc.gpsimd.tensor_tensor(w_low[:, h, cols], wfcT[:, h, cols], w_high[:, h, cols].bitcast(F32),
                                            ALU.subtract).then_inc(w_split, 1)
                gated(b, NCH - 1, PAIRS - 1)
                with pool.Fori(0, NCH) as c:
                    n = b * NCH + c
                    for j in range(JT):
                        pool.wait_ge(relu_done, done(n * JT + j + 1))
                        square = relu_ring[j % 4]
                        nc.gpsimd.tensor_tensor(square, square, square, ALU.mult).then_inc(squared, 1)

        @block.vector
        def _(dve):
            for s in DVE_SEMS:
                dve.sem_inc(s, PRIME)

            nc.vector.memset(kb[D:D + 1, :, :].bitcast(F32), 1.0).then_inc(ones_set, 1)
            nc.vector.memset(rot_sb[:, :, :], 0.0).then_inc(ones_set, 1)
            nc.vector.memset(ones[:, :], 1.0).then_inc(ones_set, 1)

            chain = [0]

            def link(ins):
                chain[0] += 1
                ins.then_inc(ln_chain, 1)
                dve.wait_ge(ln_chain, done(chain[0]))

            full, half, neg = scales[:, 0, :], scales[:, 1, :], scales[:, 2, :]

            def thresholds(cols, w, count):
                link(nc.vector.tensor_reduce(full[:, cols], w, AX_X, ALU.add, apply_absolute_value=True))
                link(nc.vector.tensor_scalar(full[:, cols], full[:, cols], 1.0 / count, 1e-5, ALU.mult, ALU.max))
                nc.vector.tensor_scalar(half[:, cols], full[:, cols], 0.5, None, ALU.mult)
                link(nc.vector.tensor_scalar(neg[:, cols], full[:, cols], -0.5, None, ALU.mult))

            def below(dst, w, q):
                return nc.vector.tensor_scalar(dst, w, neg[:, q:q + 1], None, ALU.is_lt)

            def above_less_below(dst, w, q):
                return nc.vector.scalar_tensor_tensor(out=dst, in0=w, scalar=half[:, q:q + 1], in1=dst,
                                                      op0=ALU.is_gt, op1=ALU.subtract)

            dve.wait_ge(wfc_loaded, 16)
            thresholds(slice(0, JT), wfc_nat, HID)
            for j in range(JT):
                last = below(wfc_w[:, j, :], wfc_nat[:, j, :], j)
            link(last)
            for j in range(JT):
                last = above_less_below(wfc_w[:, j, :], wfc_nat[:, j, :], j)
            link(last)
            dve.wait_ge(setup_pe, 2)
            for j in range(JT):
                last = nc.vector.scalar_tensor_tensor(
                    out=wfc_w[:, j, :], in0=wfc_w[:, j, :], scalar=full[:, j:j + 1],
                    in1=sc[:, j // 2, (j % 2) * HID:(j % 2 + 1) * HID], op0=ALU.mult, op1=ALU.add)
            last.then_inc(setup_dve, 1)
            dve.wait_ge(ffn_loaded, 16 * 6)
            thresholds(slice(JT, JT + HC), wp_nat, FFN)
            for h in range(HC):
                last = below(wp_w[:, h, :], wp_nat[:, h, :], JT + h)
                nc.vector.tensor_scalar(wp_scale[:, h * P:(h + 1) * P], ident[:, :],
                                        full[:, JT + h:JT + h + 1], None, ALU.mult)
            link(last)
            for h in range(HC):
                last = above_less_below(wp_w[:, h, :], wp_nat[:, h, :], JT + h)
            last.then_inc(setup_dve, 1)

            def reduce_max(b, c, p, j):
                unit = b * UNITS + c * PAIRS + p
                if j == 0:
                    dve.wait_ge(max8_done, done(unit - 1))
                dve.wait_ge(max_ready, done(unit * MAXES + j + 1))
                column = j % (2 * TILES) * KEYCH + j // (2 * TILES)
                nc.vector.tensor_reduce(maxp[:, p % 2, column:column + 1], mx[:, j % 2, :], AX_X, ALU.max)\
                  .then_inc(maxed, 1)

            def final_max(b, c, p):
                unit = b * UNITS + c * PAIRS + p
                dve.wait_ge(maxed, done((unit + 1) * MAXES))
                dve.wait_ge(mt_ready, done(unit))
                nc.vector.tensor_reduce(max8[:, :], maxp[:, p % 2, :].rearrange("p (q k) -> p q k", k=KEYCH),
                                        AX_X, ALU.max).then_inc(max8_done, 1)

            def copy_max(b, c, p):
                unit = b * UNITS + c * PAIRS + p
                dve.wait_ge(mt_ready, done(unit + 1))
                dve.wait_ge(m_placed, 16 * (unit + 1))
                nc.vector.tensor_scalar(mrow[:, :], misc[0:2 * TILES, 0:P], -1.0, None, ALU.mult)\
                  .then_inc(m_copied, 1)

            def fold_denominator(b, c, p):
                unit = b * UNITS + c * PAIRS + p
                dve.wait_ge(den_ready, done(unit + 1))
                dve.wait_ge(gate_copied, done(unit + 1))
                nc.vector.scalar_tensor_tensor(out=e_sb, in0=e_sb, scalar=1.0, in1=misc[:, :],
                                               op0=ALU.add, op1=ALU.mult).then_inc(den_used, 1)

            def reciprocal(b, c, p, q):
                unit, cols = b * UNITS + c * PAIRS + p, slice(q * CHUNK // PARTS, (q + 1) * CHUNK // PARTS)
                if q == 0:
                    dve.wait_ge(den_used, done(unit + 1))
                nc.vector.reciprocal(e_sb[:, cols], e_sb[:, cols]).then_inc(recip_done, 1)

            def step(b):
                def emit(c, k):
                    p, t = k // STEPS, k % STEPS

                    def look_ahead(j):
                        ahead = 1 + j // MAXES
                        if exists(c, p, ahead):
                            reduce_max(b, c, p + ahead, j % MAXES)
                            if j == MAXES - 1:
                                final_max(b, c, p + 1)

                    look_ahead(LEAD + 2 * t)
                    if t % 2 == 0:
                        look_ahead(LEAD + 2 * t + 1)
                    add_exponentials(dve, nc.vector, b, c, k, 1, sum_b)
                    if t == 2 and not first(c, p):
                        fold_denominator(b, c, p - 1)
                    if t in RECIP_STEPS and not first(c, p):
                        reciprocal(b, c, p - 1, RECIP_STEPS.index(t))
                    if t % 2:
                        look_ahead(LEAD + 2 * t + 1)
                    if t == 12 and exists(c, p, 1):
                        copy_max(b, c, p + 1)
                return emit

            LN_LINKS = 2 * TILES + 2
            setup_links = chain[0]

            def variances(count, src):
                base = setup_links + count * LN_LINKS
                end = TILES - 1
                nc.vector.bn_stats(stats[:, 0, :], src[:, 0, :]).then_inc(ln_chain, 1)
                for i in range(end):
                    dve.wait_ge(ln_chain, done(base + 2 * i + 1))
                    nc.vector.bn_stats(stats[:, i + 1, :], src[:, i + 1, :]).then_inc(ln_chain, 1)
                    nc.vector.bn_aggr(mv[:, i, :], stats[:, i, :]).then_inc(ln_chain, 1)
                dve.wait_ge(ln_chain, done(base + 2 * end + 1))
                nc.vector.tensor_scalar_add(var_eps[:, 0:end], mv[:, 0:end, 1], EPS).then_inc(ln_chain, 1)
                nc.vector.bn_aggr(mv[:, end, :], stats[:, end, :]).then_inc(ln_chain, 1)
                dve.wait_ge(ln_chain, done(base + 2 * TILES + 1))
                nc.vector.tensor_scalar_add(var_eps[:, end:TILES], mv[:, end:TILES, 1], EPS).then_inc(var_ready, 1)

            def normalise(count, src, dst, signal):
                dve.wait_ge(std_done, done(count + 1))
                nc.vector.reciprocal(rstd[:, :], std[:, :]).then_inc(ln_chain, 1)
                dve.wait_ge(ln_chain, done(setup_links + (count + 1) * LN_LINKS))
                for i in range(TILES):
                    last = nc.vector.tensor_scalar(dst[:, i, :], src[:, i, :], mv[:, i, 0:1], rstd[:, i:i + 1],
                                                   ALU.subtract, ALU.mult)
                    if signal is not None:
                        last.then_inc(signal, 1)
                return last

            def first_norm(n, c, count):
                dve.wait_ge(xres_loaded, 16 * (n + 1))
                for i in range(TILES):
                    if i % 2 == 0:
                        dve.wait_ge(tr_ready, done(2 * n + i // 2 + 1))
                    nc.vector.tensor_tensor(y1[:, i, :], sc[:, 2 + i // 2, (i % 2) * HID:(i % 2 + 1) * HID],
                                            xres[:, i, :], ALU.add).then_inc(res_done, 1)
                dve.wait_ge(res_done, done((n + 1) * TILES))
                variances(count, y1)
                normalise(count, y1, x1s[c % 2], x1_done)

            def second_sum(n, c, count):
                for i in range(TILES):
                    if i % 2 == 0:
                        dve.wait_ge(ffn2_ready, done(2 * n + i // 2 + 1))
                    bank = (ob if i < 2 else misc)[:, (i % 2) * HID:(i % 2 + 1) * HID]
                    nc.vector.tensor_tensor(y2[:, i, :], bank, wp_scale[:, :], ALU.mult).then_inc(y2_done, 1)
                for i in range(TILES):
                    dve.wait_ge(y2_done, done(n * TILES + i + 1))
                    last = nc.vector.tensor_tensor(y2[:, i, :], y2[:, i, :], x1s[c % 2][:, i, :], ALU.add)
                last.then_inc(y2_summed, 1)
                dve.wait_ge(y2_summed, done(n + 1))
                variances(count, y2)

            def second_norm(n, count):
                dve.wait_ge(y_stored, 16 * (n + 1))
                normalise(count, y2, yout, None).then_inc(post_done, 1)

            def split_x1(n):
                dve.wait_ge(ffn1_ready, done(n * JT))
                for h in range(HC):
                    dve.wait_ge(x1t_copied, done(n * HC + h + 1))
                    nc.vector.tensor_tensor(x1_low[:, h, :], sc[:, h, :], x1_high[:, h, :].bitcast(F32),
                                            ALU.subtract).then_inc(x1t_split, 1)

            def split_square(n, j):
                dve.wait_ge(sq_rounded, done(n * JT + j + 1))
                nc.vector.tensor_tensor(sq_low[:, j, :], relu_ring[j % 4], sq_high[:, j, :].bitcast(F32),
                                        ALU.subtract).then_inc(sq_split, 1)

            with dve.Fori(0, BATCH) as b:
                nc.vector.memset(probs[:, 3, :], 0.0).then_inc(rot_cleared, 1)

                def front_reduce(p, i):
                    if i == 0:
                        dve.wait_ge(max8_done, done(b * UNITS + p - 1))
                    dve.wait_ge(max_ready, done((b * UNITS + p) * MAXES + 2 * (i + 1)))
                    column = i % TILES * 2 * KEYCH + i // TILES
                    nc.vector.tensor_reduce(maxp[:, p, column:column + KEYCH + 1:KEYCH], MAX_PAIRS[i % 2], AX_X, ALU.max)\
                      .then_inc(maxed, 2)

                for s in range(PRO):
                    if FRONT[s][3] == "dve":
                        rope(nc.vector, front(s), b)
                        rope_add(nc.vector, front(s), b)
                        if FRONT[s][2] >= 2:
                            dve.wait_ge(y_stored, 16 * (NCH * b + 1))
                        rope_low(nc.vector, front(s), b)
                for i in range(MAXES // 2):
                    front_reduce(0, i)
                final_max(b, 0, 0)
                for i in range(LEAD // 2):
                    front_reduce(1, i)
                    if i == 0:
                        copy_max(b, 0, 0)
                attention_steps(dve, step(b))
                fold_denominator(b, NCH - 1, PAIRS - 1)
                for q in range(PARTS):
                    reciprocal(b, NCH - 1, PAIRS - 1, q)
                count = 2 * NCH * b
                first_norm(b * NCH, 0, count)
                for c in range(NCH):
                    n = b * NCH + c
                    split_x1(n)
                    if c >= 1:
                        second_sum(n - 1, c - 1, count + 2 * c)
                    for j in range(JT):
                        split_square(n, j)
                        if j == JT // 2 - 1 and c >= 1:
                            second_norm(n - 1, count + 2 * c)
                    if c + 1 < NCH:
                        first_norm(n + 1, c + 1, count + 2 * c + 1)
                second_sum((b + 1) * NCH - 1, NCH - 1, count + 2 * NCH - 1)
                second_norm((b + 1) * NCH - 1, count + 2 * NCH - 1)


def has_q(c, p):
    return not (isinstance(c, int) and c == NCH - 1 and p >= 1)


def raw_words(ap):
    return ap.bitcast(F32)


def head_order():
    half, rest = ROT // 2, list(range(ROT, D))
    order = []
    for i in range(half):
        order += [i] + rest[6 * i:6 * i + 3] + [half + i] + rest[6 * i + 3:6 * i + 6]
    return np.array(order)


def rotary_tables():
    inv = (np.float32(1) / np.power(10000.0, np.arange(0, ROT, 2) / ROT).astype(np.float32)).astype(np.float32)
    angle = (np.arange(SEQ, dtype=np.float32)[None, :] * inv[:, None]).astype(np.float64)
    cos, sin = np.ones((P, SEQ), np.float32), np.zeros((P, SEQ), np.float32)
    for base in (0, D):
        first_half, second_half = slice(base, base + D, 8), slice(base + 4, base + D, 8)
        cos[first_half] = cos[second_half] = np.cos(angle)
        sin[first_half], sin[second_half] = -np.sin(angle), np.sin(angle)
    return np.stack([t.reshape(P, NCH, CHUNK) for t in (cos, sin)], axis=2)


def kernel(**inputs):
    import concourse.bacc as _bacc
    from concourse.bass_utils import run_bass_kernel_spmd as _run

    a = {k: np.asarray(v) for k, v in inputs.items()}
    x = a["L0_attn_hidden_states"].reshape(BATCH * SEQ, HID)
    order = head_order()
    columns = np.concatenate([h * D + order for h in range(HEADS)] + [np.arange(HEADS * D, 2 * HEADS * D)])
    arrays = {
        "x": x, "xT": x.T, "wq": a["L0_attn_Wq"][:, columns], "wk": a["L0_attn_Wk"][:, columns[:KVH * D]], "wv": a["L0_attn_Wv"],
        "wo": a["L0_attn_Wo"], "fast_bT": a["L0_ffn_fast_b"].T, "w_fc": a["L0_ffn_w_fc"],
        "w_proj": a["L0_ffn_w_proj"], "uT": a["L0_ffn_u"].T, "v_lr": a["L0_ffn_v"],
        "gate": np.broadcast_to(a["L0_ffn_gate"].reshape(1, 1), (P, 1)),
        "tables": rotary_tables(), "ident_in": np.eye(P, dtype=np.float32),
    }
    arrays = {k: np.ascontiguousarray(v) for k, v in arrays.items()}
    nc = _bacc.Bacc("TRN2", target_bir_lowering=False, num_devices=1)
    aps = {k: nc.dram_tensor(f"in_{k}", v.shape, mybir.dt.from_np(v.dtype), kind="ExternalInput").ap()
           for k, v in arrays.items()}
    out = nc.dram_tensor("out_y", (BATCH * SEQ, HID), F32, kind="ExternalOutput").ap()
    layer_kernel(nc, out=out, **aps)
    r = _run(nc, [{f"in_{k}": v for k, v in arrays.items()}], core_ids=[0])
    return r.results[0]["out_y"].reshape(BATCH, SEQ, HID)
```
